# Optimizing a Trainium2 kernel written in Bass

```python
import numpy as np
import jax
import jax.numpy as jnp

def _softmax(x, axis=-1):
    return jax.nn.softmax(x, axis=axis)

def _gelu(x):
    return jax.nn.gelu(x, approximate=True)

def _silu(x):
    return jax.nn.silu(x)

def _sigmoid(x):
    return jax.nn.sigmoid(x)

def _layernorm(x, axis=-1, eps=1e-05):
    m = jnp.mean(x, axis=axis, keepdims=True)
    v = jnp.var(x, axis=axis, keepdims=True)
    return (x - m) / jnp.sqrt(v + eps)

def _scatter_add(tgt, idx, src, axis=0):
    return tgt.at[idx].add(src)

def _segment_sum(src, seg, n):
    return jax.ops.segment_sum(src, seg, n)
kernel_name = 'mk_xattn_ffn_d1_seqx_r4_3cdfb0'

def setup_inputs(seed: int=0):
    np.random.seed(seed)
    _w = jnp.asarray

    def _rec_inputs():
        import jax
        import jax.numpy as jnp
        _rk = jax.random.key(seed)
        x = 7.22e-05 + 1 * jax.random.normal(jax.random.fold_in(_rk, 1), (128, 128, 256), jnp.float32)
        _lenS = 128 - jax.random.randint(jax.random.fold_in(_rk, 7), (128,), 0, max(1, 128 // 4) + 1, jnp.int32)
        _lenS2 = 128 - jax.random.randint(jax.random.fold_in(_rk, 8), (128,), 0, max(1, 128 // 4) + 1, jnp.int32)
        _ctx_1024P = jax.random.normal(jax.random.fold_in(_rk, 11), (128, 16, 256), jnp.float32)
        _ctx_1024c = jax.random.dirichlet(jax.random.fold_in(_rk, 511), 0.3 * jnp.ones((16,), jnp.float32), (128, 128))
        _ctx_1024t = jnp.einsum('bsk,bkd->bsd', _ctx_1024c, _ctx_1024P)
        _ctx_1024t = _ctx_1024t * jax.lax.rsqrt(jnp.mean(jnp.square(_ctx_1024t)) + 1e-12) * 0.953939
        ctx_1024 = 4.13588e-05 + 0.999923 * (_ctx_1024t + 0.3 * jax.random.normal(jax.random.fold_in(_rk, 611), (128, 128, 256), jnp.float32))
        return (x, ctx_1024)
    x, ctx_1024 = _rec_inputs()

    def _L0_xattn_setup():
        import jax, jax.numpy as jnp
        import numpy as np
        H = 16

        def _forward(queries, keys, values, Wq, bq, Wk, bk, Wv, bv, Wo, bo):
            N, L, _ = queries.shape
            q = (queries @ Wq + bq).reshape(N, L, H, -1)
            k = (keys @ Wk + bk).reshape(N, L, H, -1)
            v = (values @ Wv + bv).reshape(N, L, H, -1)
            qp = jax.nn.elu(q) + 1.0
            kp = jax.nn.elu(k) + 1.0
            D = qp.shape[-1]
            K = v.shape[-1]

            def step(sums, inp):
                q_t, k_t, v_t = inp
                sums = sums + jnp.einsum('bhd,bhk->bhdk', k_t, v_t)
                out_t = jnp.einsum('bhdk,bhd->bhk', sums, q_t)
                return (sums, out_t)
            init = jnp.zeros((N, H, D, K), qp.dtype)
            xs = (jnp.swapaxes(qp, 0, 1), jnp.swapaxes(kp, 0, 1), jnp.swapaxes(v, 0, 1))
            _, res = jax.lax.scan(step, init, xs)
            res = jnp.swapaxes(res, 0, 1)
            Z = jnp.cumsum(qp, axis=1)
            out = (res / Z).reshape(N, L, -1)
            return out @ Wo + bo
        key = jax.random.key(seed)
        ks = jax.random.split(key, 8)
        N, L, dm = (4, 512, 256)
        scale = 0.02
        rn = lambda k, shape: jax.random.normal(k, shape, dtype=jnp.float32)
        return {'queries': rn(ks[0], (N, L, dm)), 'keys': rn(ks[1], (N, L, dm)), 'values': rn(ks[2], (N, L, dm)), 'Wq': rn(ks[3], (dm, dm)) * scale, 'bq': jnp.zeros((dm,), jnp.float32), 'Wk': rn(ks[4], (dm, dm)) * scale, 'bk': jnp.zeros((dm,), jnp.float32), 'Wv': rn(ks[5], (dm, dm)) * scale, 'bv': jnp.zeros((dm,), jnp.float32), 'Wo': rn(ks[6], (dm, dm)) * scale, 'bo': jnp.zeros((dm,), jnp.float32)}
    _L0_xattn_all = _L0_xattn_setup()
    _L0_xattn_in = {k: v for k, v in _L0_xattn_all.items() if k in ('Wq', 'bq', 'Wk', 'bk', 'Wv', 'bv', 'Wo', 'bo')}
    del _L0_xattn_all

    def _L0_ffn_setup():
        import jax, jax.numpy as jnp
        import numpy as np
        B, S, H, E = (8, 1024, 256, 8)
        TEMPERATURE = 1.0
        key = jax.random.key(seed)
        ks = jax.random.split(key, 7)
        s_h = 1.0 / np.sqrt(H).astype(np.float32)
        s_h2 = 1.0 / np.sqrt(H // 2).astype(np.float32)
        return {'hidden_states': jax.random.normal(ks[0], (B, S, H), jnp.float32), 'W1': jax.random.normal(ks[1], (H, H // 2), jnp.float32) * s_h, 'b1': jnp.zeros((H // 2,), jnp.float32), 'W2': jax.random.normal(ks[2], (H // 2, E), jnp.float32) * s_h2, 'b2': jnp.zeros((E,), jnp.float32), 'expert_W': jax.random.normal(ks[3], (E, H, H), jnp.float32) * s_h, 'expert_b': jax.random.normal(ks[4], (E, H), jnp.float32)}
    _L0_ffn_all = _L0_ffn_setup()
    _L0_ffn_in = {k: v for k, v in _L0_ffn_all.items() if k in ('W1', 'b1', 'W2', 'b2', 'expert_W', 'expert_b')}
    del _L0_ffn_all
    return {'x': x, 'ctx_1024': ctx_1024, 'L0_xattn_Wq': _L0_xattn_in['Wq'], 'L0_xattn_bq': _L0_xattn_in['bq'], 'L0_xattn_Wk': _L0_xattn_in['Wk'], 'L0_xattn_bk': _L0_xattn_in['bk'], 'L0_xattn_Wv': _L0_xattn_in['Wv'], 'L0_xattn_bv': _L0_xattn_in['bv'], 'L0_xattn_Wo': _L0_xattn_in['Wo'], 'L0_xattn_bo': _L0_xattn_in['bo'], 'L0_ffn_W1': _L0_ffn_in['W1'], 'L0_ffn_b1': _L0_ffn_in['b1'], 'L0_ffn_W2': _L0_ffn_in['W2'], 'L0_ffn_b2': _L0_ffn_in['b2'], 'L0_ffn_expert_W': _L0_ffn_in['expert_W'], 'L0_ffn_expert_b': _L0_ffn_in['expert_b']}

def reference(x, ctx_1024, L0_xattn_Wq, L0_xattn_bq, L0_xattn_Wk, L0_xattn_bk, L0_xattn_Wv, L0_xattn_bv, L0_xattn_Wo, L0_xattn_bo, L0_ffn_W1, L0_ffn_b1, L0_ffn_W2, L0_ffn_b2, L0_ffn_expert_W, L0_ffn_expert_b):
    import jax
    import jax.numpy as jnp

    def _L0_xattn_ref(queries, keys, values, Wq, bq, Wk, bk, Wv, bv, Wo, bo):
        import jax, jax.numpy as jnp
        import numpy as np
        H = 16

        def _forward(queries, keys, values, Wq, bq, Wk, bk, Wv, bv, Wo, bo):
            N, L, _ = queries.shape
            q = (queries @ Wq + bq).reshape(N, L, H, -1)
            k = (keys @ Wk + bk).reshape(N, L, H, -1)
            v = (values @ Wv + bv).reshape(N, L, H, -1)
            qp = jax.nn.elu(q) + 1.0
            kp = jax.nn.elu(k) + 1.0
            D = qp.shape[-1]
            K = v.shape[-1]

            def step(sums, inp):
                q_t, k_t, v_t = inp
                sums = sums + jnp.einsum('bhd,bhk->bhdk', k_t, v_t)
                out_t = jnp.einsum('bhdk,bhd->bhk', sums, q_t)
                return (sums, out_t)
            init = jnp.zeros((N, H, D, K), qp.dtype)
            xs = (jnp.swapaxes(qp, 0, 1), jnp.swapaxes(kp, 0, 1), jnp.swapaxes(v, 0, 1))
            _, res = jax.lax.scan(step, init, xs)
            res = jnp.swapaxes(res, 0, 1)
            Z = jnp.cumsum(qp, axis=1)
            out = (res / Z).reshape(N, L, -1)
            return out @ Wo + bo
        return _forward(queries, keys, values, Wq, bq, Wk, bk, Wv, bv, Wo, bo)

    def _L0_ffn_ref(hidden_states, W1, b1, W2, b2, expert_W, expert_b):
        import jax, jax.numpy as jnp
        import numpy as np
        B, S, H, E = (8, 1024, 256, 8)
        TEMPERATURE = 1.0
        h = jax.nn.relu(jnp.einsum('bsh,hf->bsf', hidden_states, W1) + b1)
        logits = jnp.einsum('bsf,fe->bse', h, W2) + b2
        probs = jax.nn.softmax(logits / TEMPERATURE, axis=-1)
        sel = jnp.argmax(probs, axis=-1)
        out = jnp.zeros_like(hidden_states)
        for e in range(E):
            mask = (sel == e)[..., None].astype(hidden_states.dtype)
            xe = hidden_states * mask
            ye = jnp.einsum('bsh,hd->bsd', xe, expert_W[e]) + expert_b[e]
            out = out + ye * mask
        return out
    x = x + _L0_xattn_ref(_layernorm(x, axis=-1), ctx_1024, ctx_1024, L0_xattn_Wq, L0_xattn_bq, L0_xattn_Wk, L0_xattn_bk, L0_xattn_Wv, L0_xattn_bv, L0_xattn_Wo, L0_xattn_bo)
    x = x + _L0_ffn_ref(_layernorm(x, axis=-1), L0_ffn_W1, L0_ffn_b1, L0_ffn_W2, L0_ffn_b2, L0_ffn_expert_W, L0_ffn_expert_b)
    return x

_drawn_inputs = setup_inputs


def setup_inputs(seed=0):
    import zlib

    import numpy as np

    out = dict(_drawn_inputs(seed))
    spreads = {'L0_xattn_bq': (0.0, 0.1),
     'L0_xattn_bk': (0.0, 0.1),
     'L0_xattn_bv': (0.0, 0.1),
     'L0_xattn_bo': (0.0, 0.1),
     'L0_ffn_b1': (0.0, 0.1),
     'L0_ffn_b2': (0.0, 0.1)}
    factors = {}
    for name, (base, spread) in spreads.items():
        noise = np.random.default_rng([zlib.crc32(name.encode()), seed]).standard_normal(out[name].shape)
        drawn = base * np.exp(spread * noise) if base else spread * noise
        out[name] = jnp.asarray(drawn.astype(out[name].dtype))
    for name, factor in factors.items():
        out[name] = (out[name] * factor).astype(out[name].dtype)
    return out
```

```python
import concourse.bass as bass
from concourse import mybir
from contextlib import ExitStack

F32 = mybir.dt.float32
F32R = mybir.dt.float32r
U32 = mybir.dt.uint32
ALU = mybir.AluOpType
ACT = mybir.ActivationFunctionType


def build(nc, x, ctx, wq, bq, wk, bk, wv, bv, wo, bo, w1, b1, w2, b2, we, be, out):
    TILES, P, D = x.shape
    KC = D // P
    E = we.shape[0]
    FF = w1.shape[1]
    C = 32
    NCH = P // C
    PAIRS = D // C
    HD = C // 2
    G = E // 2
    EPS = 1e-5
    MADE = KC + 5
    STAGES = 4

    with ExitStack() as stack:
        def sb(name, shape, dt=F32):
            return stack.enter_context(nc.sbuf_tensor(name, shape, dt))

        def bank(name):
            return stack.enter_context(nc.psum_tensor(name, [P, 512], F32))

        def sem(name):
            return stack.enter_context(nc.semaphore(name))

        ident = sb("ident", [P, P])
        tri = sb("tri", [P, P])
        chunk_mask = sb("chunk_mask", [P, 2 * PAIRS, C])
        head_sel = sb("head_sel", [P, 2])
        neg_half = sb("neg_half", [P, 1])
        eps_col = sb("eps_col", [P, 1])
        iota8 = sb("iota8", [P, E])
        bias_qkv = sb("bias_qkv", [P, 3 * D])
        bias_o = sb("bias_o", [P, D])
        bias_1 = sb("bias_1", [FF, 1])
        bias_2 = sb("bias_2", [P, E])
        stage_w = sb("stage_w", [P, KC, E, D])
        wqkv_hi = sb("wqkv_hi", [P, KC, 3 * D], F32R)
        wqkv_lo = sb("wqkv_lo", [P, KC, 3 * D], F32R)
        wo_hi = sb("wo_hi", [P, KC, D], F32R)
        wo_lo = sb("wo_lo", [P, KC, D], F32R)
        we_hi = sb("we_hi", [P, KC, E, D], F32R)
        we_lo = sb("we_lo", [P, KC, E, D], F32R)
        be_hi = sb("be_hi", [E, D], F32R)
        be_lo = sb("be_lo", [E, D], F32R)
        stage_be = sb("stage_be", [E, D])
        stage_small = sb("stage_small", [P, KC, 4 * D])
        w1_sb = sb("w1_sb", [P, KC, FF])
        w2_sb = sb("w2_sb", [FF, E])
        x_in = sb("x_in", [P, 2, D])
        ctx_in = sb("ctx_in", [P, 2, D])
        st1 = sb("st1", [P, 6])
        mv1 = sb("mv1", [P, 2])
        ve1 = sb("ve1", [P, 1])
        rstd1 = sb("rstd1", [P, 1])
        xn = sb("xn", [P, 2, D])
        xc_hi = sb("xc_hi", [P, 2 * D], F32R)
        xc_lo = sb("xc_lo", [P, 2 * D], F32R)
        qkv = sb("qkv", [P, 3 * D])
        qk_exp = sb("qk_exp", [P, 2 * D])
        qk_pos = sb("qk_pos", [P, 2 * D])
        qkp = sb("qkp", [P, 2 * D])
        qkT = sb("qkT", [P, 2, PAIRS, C])
        qsel = sb("qsel", [P, PAIRS, 2, C])
        state = sb("state", [P, PAIRS, C])
        scores = sb("scores", [P, PAIRS, 2, C])
        rz = sb("rz", [P, D])
        res0 = sb("res0", [P, PAIRS, C])
        resT = sb("resT", [P, PAIRS, C])
        res = sb("res", [P, D])
        att = sb("att", [P, D])
        attT_hi = sb("attT_hi", [P, D], F32R)
        attT_lo = sb("attT_lo", [P, D], F32R)
        xb = sb("xb", [P, 2, D])
        x1 = sb("x1", [P, 2, D])
        st2 = sb("st2", [P, 6])
        mv2 = sb("mv2", [P, 2])
        ve2 = sb("ve2", [P, 1])
        rstd2 = sb("rstd2", [P, 1])
        x2n = sb("x2n", [P, D])
        x2_hi = sb("x2_hi", [P, D], F32R)
        x2_lo = sb("x2_lo", [P, D], F32R)
        x2_f = sb("x2_f", [P, D])
        hT = sb("hT", [FF, P])
        logits = sb("logits", [P, E])
        top = sb("top", [P, 8])
        top_i = sb("top_i", [P, 8], U32)
        pick = sb("pick", [P, 1])
        onehot = sb("onehot", [P, E])
        onehotT = sb("onehotT", [E, P], F32R)
        acc = sb("acc", [P, 2, D])

        b_xc = bank("b_xc")
        b_ff = bank("b_ff")
        b_kv = bank("b_kv")
        b_sc = bank("b_sc")
        b_sz = bank("b_sz")
        b_o = bank("b_o")
        b_e = [bank("b_e0"), bank("b_e1")]

        s_wld = sem("s_wld")
        s_cst = sem("s_cst")
        s_split = sem("s_split")
        s_const = sem("s_const")
        s_x = [sem("s_x0"), sem("s_x1")]
        s_ctx = [sem("s_ctx0"), sem("s_ctx1")]
        s_out = [sem("s_out0"), sem("s_out1")]
        s_st1 = sem("s_st1")
        s_mv1 = sem("s_mv1")
        s_ve1 = sem("s_ve1")
        s_rstd1 = sem("s_rstd1")
        s_xn = sem("s_xn")
        s_xb = sem("s_xb")
        s_t1 = sem("s_t1")
        s_xch = sem("s_xch")
        s_xcl = sem("s_xcl")
        s_q = sem("s_q")
        s_kv = sem("s_kv")
        s_qb = sem("s_qb")
        s_kvb = sem("s_kvb")
        s_exp = sem("s_exp")
        s_pos = sem("s_pos")
        s_qkp = sem("s_qkp")
        s_qkT = sem("s_qkT")
        s_qsel = sem("s_qsel")
        s_sz = sem("s_sz")
        s_sc = sem("s_sc")
        s_state = sem("s_state")
        s_scores = sem("s_scores")
        s_rz = sem("s_rz")
        s_o = sem("s_o")
        s_res0 = sem("s_res0")
        s_resT = sem("s_resT")
        s_res = sem("s_res")
        s_att = sem("s_att")
        s_attT = sem("s_attT")
        s_ath = sem("s_ath")
        s_atl = sem("s_atl")
        s_y = sem("s_y")
        s_x1s = sem("s_x1s")
        s_st2 = sem("s_st2")
        s_mv2 = sem("s_mv2")
        s_ve2 = sem("s_ve2")
        s_rstd2 = sem("s_rstd2")
        s_x2n = sem("s_x2n")
        s_x2T = sem("s_x2T")
        s_x2h = sem("s_x2h")
        s_x2l = sem("s_x2l")
        s_hid = sem("s_hid")
        s_hT = sem("s_hT")
        s_lgp = sem("s_lgp")
        s_pick = sem("s_pick")
        s_hot = sem("s_hot")
        s_hotT = sem("s_hotT")
        s_hotc = sem("s_hotc")
        s_be = sem("s_be")
        s_acc = sem("s_acc")
        s_e = sem("s_e")
        s_efree = sem("s_efree")

        block = stack.enter_context(nc.Block())

        def n(t, per=1, k=0):
            i, d = t
            return 2 * per * i + per * d + k

        def half(t):
            i, d = t
            return i + d // 2

        def slot(t):
            return t[1] % 2

        def schedule(eng, step):
            def one(i, u, live):
                step(*((i, u - k) if live(k) else None for k in range(STAGES)))
            lead = STAGES + STAGES % 2
            for j in range(lead):
                one(j // 2, j % 2, lambda k: j - k >= 0)
            with eng.Fori(lead // 2, TILES // 2, 1) as i:
                for u in range(2):
                    one(i, u, lambda k: True)
            for j in range(TILES, TILES + STAGES - 1):
                one(j // 2, j % 2, lambda k: j - k < TILES)

        def first(t):
            return isinstance(t[0], int) and 2 * t[0] + t[1] == 0

        def tile_no(t):
            return 2 * t[0] + t[1] if isinstance(t[0], int) else None

        def of(dram, t):
            return dram.rearrange("(i u) p n -> i u p n", u=2)[bass.ds(half(t), 1), slot(t), :, :]\
                .rearrange("o p n -> (o p) n")

        @block.sync
        def _(sp):
            for k, w in enumerate((wq, wk, wv, wo)):
                sp.dma_start(stage_small[:, :, k * D:(k + 1) * D],
                             w.rearrange("(k p) n -> p k n", p=P)).then_inc(s_wld, 16)
            for e in range(E):
                sp.dma_start(stage_w[:, :, e, :], we[e, :, :].rearrange("(k p) n -> p k n", p=P)).then_inc(s_wld, 16)
            sp.dma_start(w1_sb[:, :, :], w1.rearrange("(k p) n -> p k n", p=P)).then_inc(s_wld, 16)
            sp.dma_start(w2_sb[:, :], w2).then_inc(s_wld, 16)
            sp.dma_start(stage_be[:, :], be).then_inc(s_wld, 16)
            for k, b in enumerate((bq, bk, bv)):
                sp.dma_start(bias_qkv[:, k * D:(k + 1) * D],
                             b.rearrange("(o n) -> o n", o=1).to_broadcast((P, D))).then_inc(s_wld, 16)
            sp.dma_start(bias_o[:, :], bo.rearrange("(o n) -> o n", o=1).to_broadcast((P, D))).then_inc(s_wld, 16)
            sp.dma_start(bias_1[:, :], b1.rearrange("(n o) -> n o", o=1)).then_inc(s_wld, 16)
            sp.dma_start(bias_2[:, :], b2.rearrange("(o n) -> o n", o=1).to_broadcast((P, E))).then_inc(s_wld, 16)

            def load_x(t):
                if not (tile_no(t) is not None and tile_no(t) < 2):
                    sp.wait_ge(s_xb, n(t, k=-1))
                    sp.wait_ge(s_xn, n(t, k=-1))
                sp.dma_start(x_in[:, slot(t), :], of(x, t)).then_inc(s_x[slot(t)], 16)

            def load_ctx(t):
                if not (tile_no(t) is not None and tile_no(t) < 2):
                    sp.wait_ge(s_t1, n(t, k=-1))
                sp.dma_start(ctx_in[:, slot(t), :], of(ctx, t)).then_inc(s_ctx[slot(t)], 16)

            def step(norm, project, attend, experts):
                if norm:
                    load_x(norm)
                    load_ctx(norm)
                if experts:
                    sp.wait_ge(s_acc, n(experts, E + 1, E + 1))
                    sp.dma_start(of(out, experts), acc[:, slot(experts), :]).then_inc(s_out[slot(experts)], 16)

            schedule(sp, step)
            for s in range(2):
                sp.wait_ge(s_out[s], 16 * (TILES // 2))

        @block.gpsimd
        def _(pool):
            pool.memset(ident[:, :], 0.0).then_inc(s_const, 1)
            pool.memset(tri[:, :], 1.0).then_inc(s_const, 1)
            pool.memset(neg_half[:, :], -0.5).then_inc(s_const, 1)
            pool.memset(eps_col[:, :], EPS).then_inc(s_const, 1)
            pool.iota(iota8[:, :], pattern=[[1, E]], base=0, channel_multiplier=0,
                      allow_small_or_imprecise_dtypes=True).then_inc(s_const, 1)
            pool.wait_ge(s_const, 5)
            pool.affine_select(out=ident[:, :], in_=ident[:, :], compare_op=ALU.not_equal, fill=1.0,
                               base=0, pattern=[[-1, P]], channel_multiplier=1).then_inc(s_const, 1)
            pool.affine_select(out=tri[:, :], in_=tri[:, :], compare_op=ALU.is_ge, fill=0.0,
                               base=0, pattern=[[1, P]], channel_multiplier=-1).then_inc(s_const, 1)
            pool.wait_ge(s_wld, 16 * (4 + E + 3 + 6))

            def step(norm, project, attend, experts):
                if project:
                    if not (tile_no(project) is not None and tile_no(project) < 2):
                        pool.wait_ge(s_x1s, n(project, k=-1))
                    pool.wait_ge(s_x[slot(project)], 16 * half(project) + 16)
                    pool.tensor_tensor(xb[:, slot(project), :], x_in[:, slot(project), :], bias_o[:, :],
                                       ALU.add).then_inc(s_xb, 1)
                if norm:
                    pool.wait_ge(s_mv1, n(norm, k=1))
                    pool.tensor_tensor(ve1[:, :], mv1[:, 1:2], eps_col[:, :], ALU.add).then_inc(s_ve1, 1)
                    pool.wait_ge(s_ve1, n(norm, k=1))
                    pool.tensor_tensor(rstd1[:, :], ve1[:, :], neg_half[:, :], ALU.pow).then_inc(s_rstd1, 1)
                if attend:
                    pool.wait_ge(s_res, n(attend, k=1))
                    pool.wait_ge(s_rz, n(attend, k=1))
                    pool.tensor_tensor(att[:, :], res[:, :], rz[:, :], ALU.mult).then_inc(s_att, 1)
                if attend:
                    pool.wait_ge(s_mv2, n(attend, k=1))
                    pool.tensor_tensor(ve2[:, :], mv2[:, 1:2], eps_col[:, :], ALU.add).then_inc(s_ve2, 1)
                    pool.wait_ge(s_ve2, n(attend, k=1))
                    pool.tensor_tensor(rstd2[:, :], ve2[:, :], neg_half[:, :], ALU.pow).then_inc(s_rstd2, 1)

            schedule(pool, step)

        @block.scalar
        def _(act):
            act.wait_ge(s_wld, 16 * (4 + E + 3 + 6))
            act.activation(wqkv_hi[:, :, :], stage_small[:, :, 0:3 * D], ACT.Copy).then_inc(s_split, 1)
            act.activation(wo_hi[:, :, :], stage_small[:, :, 3 * D:4 * D], ACT.Copy).then_inc(s_split, 1)
            act.activation(be_hi[:, :], stage_be[:, :], ACT.Copy).then_inc(s_split, 1)
            for k in range(KC):
                act.activation(we_hi[:, k, :, :], stage_w[:, k, :, :], ACT.Copy).then_inc(s_split, 1)
            act.wait_ge(s_cst, 1)

            def step(norm, project, attend, experts):
                if project:
                    act.wait_ge(s_t1, n(project, k=1))
                    act.activation(xc_hi[:, :], b_xc[:, :], ACT.Copy).then_inc(s_xch, 1)
                if attend:
                    act.wait_ge(s_sz, n(attend, k=1))
                    act.activation(state[C:2 * C, :, :], b_sz[C:2 * C, 0:D].rearrange("p (a b) -> p a b", b=C),
                                   ACT.Copy).then_inc(s_state, 1)
                    act.activation(state[2 * C:P, :, :], b_sz[2 * C:P, 0:D].rearrange("p (a b) -> p a b", b=C),
                                   ACT.Copy).then_inc(s_state, 1)
                if experts:
                    act.wait_ge(s_x2T, n(experts, k=1))
                    act.activation(x2_hi[:, :], b_ff[:, 0:D], ACT.Copy).then_inc(s_x2h, 1)
                    act.activation(x2_f[:, :], b_ff[:, 0:D], ACT.Copy).then_inc(s_x2h, 1)
                if experts:
                    act.wait_ge(s_hid, n(experts, k=1))
                    act.activation(hT[:, :], b_ff[0:FF, D:D + P], ACT.Relu, bias=bias_1[:, :]).then_inc(s_hT, 1)
                if attend:
                    act.wait_ge(s_o, n(attend, k=1))
                    act.activation(res0[:, :, :],
                                   b_o[:, :].rearrange("p (a h b) -> p a h b", h=2, b=C)[:, :, 0, :],
                                   ACT.Copy, scale=head_sel[:, 0:1]).then_inc(s_res0, 1)
                if experts:
                    act.wait_ge(s_hotT, n(experts, k=1))
                    act.activation(onehotT[:, :], b_ff[0:E, 0:P], ACT.Copy).then_inc(s_hotc, 1)
                if project:
                    act.wait_ge(s_kvb, n(project, k=1))
                    act.activation(qk_exp[:, :], qkv[:, 0:2 * D], ACT.Exp).then_inc(s_exp, 1)
                    act.activation(qk_pos[:, :], qkv[:, 0:2 * D], ACT.Relu).then_inc(s_pos, 1)
                    act.wait_ge(s_qkT, n(project, k=1))
                    for h in range(2):
                        act.activation(qsel[:, :, h, :], qkT[:, 0, :, :], ACT.Copy,
                                       scale=head_sel[:, h:h + 1]).then_inc(s_qsel, 1)
                if attend:
                    act.wait_ge(s_attT, n(attend, k=1))
                    act.activation(attT_hi[:, :], b_sc[:, 0:D], ACT.Copy).then_inc(s_ath, 1)

            schedule(act, step)

        @block.vector
        def _(dve):
            dve.memset(head_sel[:, 0:1], 0.0).then_inc(s_split, 1)
            dve.memset(head_sel[:, 1:2], 1.0).then_inc(s_split, 1)
            dve.wait_ge(s_split, KC + 5)
            for c in range(NCH):
                dve.memset(head_sel[C * c:C * c + HD, 0:1], 1.0)
                last = dve.memset(head_sel[C * c:C * c + HD, 1:2], 0.0)
            last.then_inc(s_cst, 1)
            dve.tensor_tensor(wqkv_lo[:, :, :], stage_small[:, :, 0:3 * D], wqkv_hi[:, :, :].bitcast(F32),
                              ALU.subtract).then_inc(s_cst, 1)
            dve.tensor_tensor(wo_lo[:, :, :], stage_small[:, :, 3 * D:4 * D], wo_hi[:, :, :].bitcast(F32),
                              ALU.subtract).then_inc(s_cst, 1)
            dve.tensor_tensor(be_lo[:, :], stage_be[:, :], be_hi[:, :].bitcast(F32), ALU.subtract).then_inc(s_cst, 1)
            for k in range(KC):
                dve.tensor_tensor(we_lo[:, k, :, :], stage_w[:, k, :, :], we_hi[:, k, :, :].bitcast(F32),
                                  ALU.subtract).then_inc(s_cst, 1)
            dve.wait_ge(s_const, 7)
            for c in range(NCH):
                for h in range(2 * PAIRS):
                    last = dve.tensor_copy(chunk_mask[C * c:C * c + C, h, :], tri[C * c:C * c + C, C * c:C * c + C])
            last.then_inc(s_cst, 1)
            dve.wait_ge(s_cst, MADE)

            def experts_group(t, g):
                dve.wait_ge(s_e, n(t, G, g + 1))
                for h in range(2):
                    e = 2 * g + h
                    dve.wait_ge(s_acc, n(t, E + 1, e + 1))
                    ins = dve.scalar_tensor_tensor(acc[:, slot(t), :], b_e[g % 2][:, h * D:(h + 1) * D],
                                                   onehot[:, e:e + 1], acc[:, slot(t), :], ALU.mult, ALU.add)
                    ins.then_inc(s_acc, 1)
                dve.wait_ge(s_acc, n(t, E + 1, 2 * g + 3))
                dve.sem_inc(s_efree, 1)

            def step(norm, project, attend, experts):
                if project:
                    dve.wait_ge(s_xch, n(project, k=1))
                    dve.tensor_tensor(xc_lo[:, :], b_xc[:, :], xc_hi[:, :].bitcast(F32), ALU.subtract).then_inc(s_xcl, 1)
                if norm:
                    dve.wait_ge(s_x[slot(norm)], 16 * half(norm) + 16)
                    dve.bn_stats(st1[:, :], x_in[:, slot(norm), :]).then_inc(s_st1, 1)
                    dve.wait_ge(s_st1, n(norm, k=1))
                if attend:
                    dve.wait_ge(s_sc, n(attend, k=1))
                    dve.tensor_tensor(scores[:, :, :, :].rearrange("p a h b -> p (a h b)"), b_sc[:, :],
                                      chunk_mask[:, :, :].rearrange("p a b -> p (a b)"), ALU.mult).then_inc(s_scores, 1)
                if norm:
                    dve.bn_aggr(mv1[:, :], st1[:, :]).then_inc(s_mv1, 1)
                if experts:
                    dve.wait_ge(s_x2h, n(experts, 2, 2))
                    dve.tensor_tensor(x2_lo[:, :], b_ff[:, 0:D], x2_hi[:, :].bitcast(F32), ALU.subtract).then_inc(s_x2l, 1)
                if attend:
                    dve.wait_ge(s_state, n(attend, 2, 2))
                    dve.reciprocal(rz[:, :], b_sz[:, D:2 * D]).then_inc(s_rz, 1)
                if experts:
                    dve.wait_ge(s_lgp, n(experts, k=1))
                    dve.tensor_tensor(logits[:, :], b_ff[:, D + P:D + P + E], bias_2[:, :], ALU.add).then_inc(s_pick, 1)
                    dve.wait_ge(s_pick, n(experts, 4, 1))
                if attend:
                    dve.wait_ge(s_res0, n(attend, k=1))
                    dve.scalar_tensor_tensor(resT[:, :, :],
                                             b_o[:, :].rearrange("p (a h b) -> p a h b", h=2, b=C)[:, :, 1, :],
                                             head_sel[:, 1:2], res0[:, :, :], ALU.mult, ALU.add).then_inc(s_resT, 1)
                if experts:
                    dve.max(top[:, :], logits[:, :]).then_inc(s_pick, 1)
                    dve.wait_ge(s_pick, n(experts, 4, 2))
                if attend:
                    dve.wait_ge(s_resT, n(attend, k=1))
                    dve.transpose(res[:, :], resT[:, :, :].rearrange("p a b -> p (a b)")).then_inc(s_res, 1)
                if experts:
                    dve.max_index(top_i[:, :], top[:, :], logits[:, :]).then_inc(s_pick, 1)
                    dve.wait_ge(s_pick, n(experts, 4, 3))
                    dve.tensor_copy(pick[:, :], top_i[:, 0:1]).then_inc(s_pick, 1)
                    dve.wait_ge(s_pick, n(experts, 4, 4))
                    dve.tensor_scalar(onehot[:, :], iota8[:, :], pick[:, 0:1], None, ALU.is_equal).then_inc(s_hot, 1)
                if norm:
                    dve.wait_ge(s_rstd1, n(norm, k=1))
                    if not (tile_no(norm) is not None and tile_no(norm) < 2):
                        dve.wait_ge(s_t1, n(norm, k=-1))
                    dve.tensor_scalar(xn[:, slot(norm), :], x_in[:, slot(norm), :], mv1[:, 0:1], rstd1[:, 0:1],
                                      ALU.subtract, ALU.mult).then_inc(s_xn, 1)
                if project:
                    dve.wait_ge(s_q, n(project, k=1))
                    dve.tensor_tensor(qkv[:, 0:D], b_xc[:, 0:D], bias_qkv[:, 0:D], ALU.add).then_inc(s_qb, 1)
                    dve.wait_ge(s_kv, n(project, k=1))
                    dve.tensor_tensor(qkv[:, D:3 * D], b_kv[:, :], bias_qkv[:, D:3 * D], ALU.add).then_inc(s_kvb, 1)
                if experts:
                    dve.wait_ge(s_be, n(experts, k=1))
                    if not (tile_no(experts) is not None and tile_no(experts) < 2):
                        dve.wait_ge(s_out[slot(experts)], 16 * half(experts))
                    dve.tensor_tensor(acc[:, slot(experts), :], b_ff[:, D:2 * D], x1[:, slot(experts), :],
                                      ALU.add).then_inc(s_acc, 1)
                    experts_group(experts, 0)
                if project:
                    dve.wait_ge(s_exp, n(project, k=1))
                    dve.wait_ge(s_pos, n(project, k=1))
                    dve.scalar_tensor_tensor(qkp[:, :], qk_exp[:, :], 1.0, qk_pos[:, :], ALU.min, ALU.add).then_inc(s_qkp, 1)
                    dve.wait_ge(s_qkp, n(project, k=1))
                    dve.transpose(qkT[:, :, :, :].rearrange("p q a b -> p (q a b)"), qkp[:, :]).then_inc(s_qkT, 1)
                if attend:
                    dve.wait_ge(s_ath, n(attend, k=1))
                    dve.tensor_tensor(attT_lo[:, :], b_sc[:, 0:D], attT_hi[:, :].bitcast(F32), ALU.subtract).then_inc(s_atl, 1)
                if experts:
                    experts_group(experts, 1)
                if attend:
                    dve.wait_ge(s_y, n(attend, k=1))
                    dve.wait_ge(s_xb, n(attend, k=1))
                    dve.tensor_tensor(x1[:, slot(attend), :], b_sz[:, 0:D], xb[:, slot(attend), :], ALU.add).then_inc(s_x1s, 1)
                    dve.wait_ge(s_x1s, n(attend, k=1))
                    dve.bn_stats(st2[:, :], x1[:, slot(attend), :]).then_inc(s_st2, 1)
                    dve.wait_ge(s_st2, n(attend, k=1))
                if experts:
                    experts_group(experts, 2)
                if attend:
                    dve.bn_aggr(mv2[:, :], st2[:, :]).then_inc(s_mv2, 1)
                if experts:
                    experts_group(experts, 3)
                if attend:
                    dve.wait_ge(s_rstd2, n(attend, k=1))
                    dve.tensor_scalar(x2n[:, :], x1[:, slot(attend), :], mv2[:, 0:1], rstd2[:, 0:1],
                                      ALU.subtract, ALU.mult).then_inc(s_x2n, 1)

            schedule(dve, step)

        @block.tensor
        def _(pe):
            pe.wait_ge(s_const, 7)
            pe.wait_ge(s_cst, MADE)
            pe.wait_ge(s_wld, 16 * (4 + E + 3 + 6))

            def split_product(dst, lhs_hi, lhs_lo, rhs_hi, rhs_lo):
                parts = [(k, a, b) for k in range(KC) for a, b in
                         ((lhs_hi, rhs_hi), (lhs_hi, rhs_lo), (lhs_lo, rhs_hi))]
                for m, (k, a, b) in enumerate(parts):
                    last = pe.matmul(dst, a(k), b(k), start=(m == 0), stop=(m == len(parts) - 1))
                return last

            def expert_pair(t, g):
                if not (first(t) and g < 2):
                    pe.wait_ge(s_efree, n(t, G, g - 1))
                split_product(b_e[g % 2][:, :],
                              lambda k: x2_hi[:, k * P:(k + 1) * P], lambda k: x2_lo[:, k * P:(k + 1) * P],
                              lambda k: we_hi[:, k, 2 * g:2 * g + 2, :], lambda k: we_lo[:, k, 2 * g:2 * g + 2, :])\
                    .then_inc(s_e, 1)

            def rows(c):
                return slice(C * c, C * c + C)

            def step(norm, project, attend, experts):
                if project:
                    pe.wait_ge(s_xn, n(project, k=1))
                    pe.wait_ge(s_ctx[slot(project)], 16 * half(project) + 16)
                    if not first(project):
                        pe.wait_ge(s_qb, n(project))
                    for k in range(KC):
                        pe.transpose(b_xc[:, k * P:(k + 1) * P], xn[:, slot(project), k * P:(k + 1) * P], ident[:, :])
                    for k in range(KC):
                        last = pe.transpose(b_xc[:, D + k * P:D + (k + 1) * P],
                                            ctx_in[:, slot(project), k * P:(k + 1) * P], ident[:, :])
                    last.then_inc(s_t1, 1)
                if attend:
                    pe.wait_ge(s_qsel, n(attend, 2, 2))
                    if not first(attend):
                        pe.wait_ge(s_x1s, n(attend))
                        pe.wait_ge(s_atl, n(attend))
                    pe.matmul(b_sz[:, D:2 * D], tri[:, :], qkp[:, 0:D], start=True, stop=True)
                    for p in range(PAIRS):
                        for c in range(1, NCH):
                            f = slice(C * p, C * p + C)
                            last = pe.matmul(b_sz[rows(c), C * p:C * p + C],
                                             qkp[0:C * c, D + C * p:D + C * p + C],
                                             qkv[0:C * c, 2 * D + C * p:2 * D + C * p + C], start=True, stop=True)
                    last.then_inc(s_sz, 1)
                    for p in range(PAIRS):
                        for c in range(NCH):
                            last = pe.matmul(b_sc[rows(c), 2 * C * p:2 * C * (p + 1)], qkT[rows(c), 1, p, :],
                                             qsel[rows(c), p, :, :], start=True, stop=True)
                    last.then_inc(s_sc, 1)
                if experts:
                    pe.wait_ge(s_x2n, n(experts, k=1))
                    if not first(experts):
                        pe.wait_ge(s_acc, n(experts, E + 1, -E))
                    for k in range(KC):
                        last = pe.transpose(b_ff[:, k * P:(k + 1) * P], x2n[:, k * P:(k + 1) * P], ident[:, :])
                    last.then_inc(s_x2T, 1)
                if experts:
                    pe.wait_ge(s_x2l, n(experts, k=1))
                    for k in range(KC):
                        last = pe.matmul(b_ff[0:FF, D:D + P], w1_sb[:, k, :], x2_f[:, k * P:(k + 1) * P],
                                         start=(k == 0), stop=(k == KC - 1))
                    last.then_inc(s_hid, 1)
                    expert_pair(experts, 0)
                if attend:
                    pe.wait_ge(s_cst, MADE)
                    pe.wait_ge(s_state, n(attend, 2, 2))
                    pe.wait_ge(s_scores, n(attend, k=1))
                    if not first(attend):
                        pe.wait_ge(s_resT, n(attend))
                    for p in range(PAIRS):
                        for c in range(NCH):
                            last = pe.matmul(b_o[rows(c), 2 * C * p:2 * C * (p + 1)],
                                             qkv[rows(c), 2 * D + C * p:2 * D + C * p + C],
                                             scores[rows(c), p, :, :], start=True, stop=(c == 0))
                        for c in range(1, NCH):
                            last = pe.matmul(b_o[rows(c), 2 * C * p:2 * C * (p + 1)], state[rows(c), p, :],
                                             qsel[rows(c), p, :, :], start=False, stop=True)
                    last.then_inc(s_o, 1)
                if experts:
                    pe.wait_ge(s_hT, n(experts, k=1))
                    pe.matmul(b_ff[:, D + P:D + P + E], hT[:, :], w2_sb[:, :], start=True, stop=True).then_inc(s_lgp, 1)
                if project:
                    pe.wait_ge(s_xcl, n(project, k=1))
                    split_product(b_xc[:, 0:D],
                                  lambda k: xc_hi[:, k * P:(k + 1) * P], lambda k: xc_lo[:, k * P:(k + 1) * P],
                                  lambda k: wqkv_hi[:, k, 0:D], lambda k: wqkv_lo[:, k, 0:D]).then_inc(s_q, 1)
                    if not first(project):
                        pe.wait_ge(s_kvb, n(project))
                    split_product(b_kv[:, :],
                                  lambda k: xc_hi[:, D + k * P:D + (k + 1) * P], lambda k: xc_lo[:, D + k * P:D + (k + 1) * P],
                                  lambda k: wqkv_hi[:, k, D:3 * D], lambda k: wqkv_lo[:, k, D:3 * D]).then_inc(s_kv, 1)
                if experts:
                    pe.wait_ge(s_hot, n(experts, k=1))
                    pe.transpose(b_ff[0:E, 0:P], onehot[:, :], ident[:, :]).then_inc(s_hotT, 1)
                if attend:
                    pe.wait_ge(s_att, n(attend, k=1))
                    for k in range(KC):
                        last = pe.transpose(b_sc[:, k * P:(k + 1) * P], att[:, k * P:(k + 1) * P], ident[:, :])
                    last.then_inc(s_attT, 1)
                if experts:
                    expert_pair(experts, 1)
                    pe.wait_ge(s_hotc, n(experts, k=1))
                    pe.matmul(b_ff[:, D:2 * D], onehotT[:, :], be_hi[:, :], start=True, stop=False)
                    pe.matmul(b_ff[:, D:2 * D], onehotT[:, :], be_lo[:, :], start=False, stop=True).then_inc(s_be, 1)
                if attend:
                    pe.wait_ge(s_atl, n(attend, k=1))
                    split_product(b_sz[:, 0:D],
                                  lambda k: attT_hi[:, k * P:(k + 1) * P], lambda k: attT_lo[:, k * P:(k + 1) * P],
                                  lambda k: wo_hi[:, k, :], lambda k: wo_lo[:, k, :]).then_inc(s_y, 1)
                if experts:
                    expert_pair(experts, 2)
                    expert_pair(experts, 3)

            schedule(pe, step)


_INS = ["x", "ctx_1024", "L0_xattn_Wq", "L0_xattn_bq", "L0_xattn_Wk", "L0_xattn_bk", "L0_xattn_Wv",
        "L0_xattn_bv", "L0_xattn_Wo", "L0_xattn_bo", "L0_ffn_W1", "L0_ffn_b1", "L0_ffn_W2", "L0_ffn_b2",
        "L0_ffn_expert_W", "L0_ffn_expert_b"]


def kernel(**inputs):
    import numpy as np
    import concourse.bacc as bacc
    from concourse.bass_utils import run_bass_kernel_spmd

    nc = bacc.Bacc("TRN2", target_bir_lowering=False, num_devices=1)
    arrays, args = {}, []
    for name in _INS:
        a = np.ascontiguousarray(inputs[name])
        arrays[f"in_{name}"] = a
        args.append(nc.dram_tensor(f"in_{name}", a.shape, mybir.dt.from_np(a.dtype), kind="ExternalInput").ap())
    out = nc.dram_tensor("out", arrays["in_x"].shape, F32, kind="ExternalOutput").ap()
    build(nc, *args, out)
    return run_bass_kernel_spmd(nc, [arrays], core_ids=[0]).results[0]["out"]
```

```python
import concourse.bass as bass
from concourse import mybir
from contextlib import ExitStack

F32 = mybir.dt.float32
F32R = mybir.dt.float32r
BF16 = mybir.dt.bfloat16
U32 = mybir.dt.uint32
I32 = mybir.dt.int32
ALU = mybir.AluOpType
ACT = mybir.ActivationFunctionType


def build(nc, x, ctx, wq, bq, wk, bk, wv, bv, wo, bo, w1, b1, w2, b2, we, be, out):
    TILES, P, D = x.shape
    KC = D // P
    E = we.shape[0]
    FF = w1.shape[1]
    C = 32
    NCH = P // C
    PAIRS = D // C
    HD = C // 2
    EPS = 1e-5
    TOKENS = TILES * P
    CAP = TOKENS + P
    SPARE = E * CAP
    ROW = D + 4
    MEAN, RSTD, TOKEN = D, D + 2, D + 3
    NOBODY = 1 << 20
    SLOTS = TILES + E
    STAGES = 5
    RING = 8
    WEIGHTS = 16 * (4 + E + 3 + 6)
    POOL_MADE = 18
    MADE = KC + 8
    FILL_STEPS = E + 4 + 3 * (E - 1) + 4

    with ExitStack() as stack:
        def sb(name, shape, dt=F32):
            return stack.enter_context(nc.sbuf_tensor(name, shape, dt))

        def bank(name):
            return stack.enter_context(nc.psum_tensor(name, [P, 512], F32))

        def sem(name):
            return stack.enter_context(nc.semaphore(name))

        buckets = nc.dram_tensor("buckets", (SPARE + P, ROW), F32, kind="Internal").ap()

        ident = sb("ident", [P, P])
        tri = sb("tri", [P, P])
        before = sb("before", [P, P], BF16)
        ones = sb("ones", [P, P], BF16)
        chunk_mask = sb("chunk_mask", [P, 2 * PAIRS, C])
        head_sel = sb("head_sel", [P, 2])
        neg_half = sb("neg_half", [P, 1])
        eps_col = sb("eps_col", [P, 1])
        iota8 = sb("iota8", [P, E])
        tokens = sb("tokens", [P, TILES], U32)
        pad_row = sb("pad_row", [P, ROW])
        pad_at = sb("pad_at", [P, E])
        multiples = sb("multiples", [1, TILES])
        slot_no = sb("slot_no", [1, SLOTS])
        zero_u = sb("zero_u", [P, 1], U32)
        bias_qkv = sb("bias_qkv", [P, 3 * D])
        bias_o = sb("bias_o", [P, D])
        bias_1 = sb("bias_1", [FF, 1])
        bias_2 = sb("bias_2", [P, E])
        stage_w = sb("stage_w", [P, KC, E, D])
        wqkv_hi = sb("wqkv_hi", [P, KC, 3 * D], F32R)
        wqkv_lo = sb("wqkv_lo", [P, KC, 3 * D], F32R)
        wo_hi = sb("wo_hi", [P, KC, D], F32R)
        wo_lo = sb("wo_lo", [P, KC, D], F32R)
        we_hi = sb("we_hi", [P, KC, E, D], F32R)
        we_lo = sb("we_lo", [P, KC, E, D], F32R)
        be_hi = sb("be_hi", [1, E, D], F32R)
        be_lo = sb("be_lo", [1, E, D], F32R)
        stage_be = sb("stage_be", [1, E, D])
        ones_row = sb("ones_row", [1, P], F32R)
        stage_small = sb("stage_small", [P, KC, 4 * D])
        w1_sb = sb("w1_sb", [P, KC, FF])
        w2_sb = sb("w2_sb", [FF, E])
        x_in = sb("x_in", [P, 2, D])
        ctx_in = sb("ctx_in", [P, 2, D])
        st1 = sb("st1", [P, 6])
        mv1 = sb("mv1", [P, 2])
        ve1 = sb("ve1", [P, 1])
        rstd1 = sb("rstd1", [P, 1])
        xn = sb("xn", [P, D])
        xc_hi = sb("xc_hi", [P, 2 * D], F32R)
        xc_lo = sb("xc_lo", [P, 2 * D], F32R)
        qk = sb("qk", [P, 2 * D])
        v = sb("v", [P, 2, D])
        qk_exp = sb("qk_exp", [P, 2 * D])
        qk_pos = sb("qk_pos", [P, 2 * D])
        qkp = sb("qkp", [P, 2 * D])
        qkT = sb("qkT", [P, 2, PAIRS, C])
        qsel = sb("qsel", [P, 2, PAIRS, 2, C])
        state = sb("state", [P, PAIRS, C])
        scores = sb("scores", [P, PAIRS, 2, C])
        z = sb("z", [P, D])
        z_ln = sb("z_ln", [P, D])
        z_inv = sb("z_inv", [P, D])
        z_prod = sb("z_prod", [P, D])
        rz = sb("rz", [P, D])
        res0 = sb("res0", [P, PAIRS, C])
        resT = sb("resT", [P, PAIRS, C])
        res = sb("res", [P, D])
        att = sb("att", [P, D])
        attT_hi = sb("attT_hi", [P, D], F32R)
        attT_lo = sb("attT_lo", [P, D], F32R)
        xb = sb("xb", [P, 2, D])
        row = sb("row", [P, 2, ROW])
        st2 = sb("st2", [P, 6])
        ve2 = sb("ve2", [P, 1])
        x2n = sb("x2n", [P, D])
        x2_f = sb("x2_f", [P, D])
        hT = sb("hT", [FF, P])
        logits = sb("logits", [P, E])
        top = sb("top", [P, 8])
        pick = sb("pick", [P, 8], U32)
        onehot = sb("onehot", [P, E], BF16)
        onehots = sb("onehots", [P, E], BF16)
        ranked = sb("ranked", [P, E])
        rank = sb("rank", [P, 1])
        place = sb("place", [P, 2], U32)
        count = sb("count", [P, E])
        pad_place = sb("pad_place", [P, E], U32)
        over = sb("over", [1, TILES])
        fill = sb("fill", [1, E])
        fill_sum = sb("fill_sum", [1, E])
        one_e = sb("one_e", [1, E])
        jump = sb("jump", [1, E])
        step_row = sb("step_row", [1, SLOTS])
        slot_e = sb("slot_e", [1, SLOTS])
        slot_row = sb("slot_row", [1, SLOTS])
        slot_used = sb("slot_used", [1, SLOTS])
        expert_of = sb("expert_of", [1, SLOTS], I32)
        row_of = sb("row_of", [1, SLOTS], I32)
        rows2 = sb("rows2", [P, RING, ROW])
        x3n = sb("x3n", [P, 2, D])
        x3_hi = sb("x3_hi", [P, 2, D], F32R)
        x3_lo = sb("x3_lo", [P, 2, D], F32R)
        sums = sb("sums", [P, RING, D])
        token = sb("token", [P, RING], U32)

        b_xc = bank("b_xc")
        b_q = bank("b_q")
        b_kv = bank("b_kv")
        b_sc = bank("b_sc")
        b_st = bank("b_st")
        b_z = bank("b_z")
        b_o = bank("b_o")

        s_wld = sem("s_wld")
        s_cst = sem("s_cst")
        s_hi = sem("s_hi")
        s_const = sem("s_const")
        s_x = [sem("s_x0"), sem("s_x1")]
        s_ctx = [sem("s_ctx0"), sem("s_ctx1")]
        s_bucket = [sem("s_bucket0"), sem("s_bucket1")]
        s_pad = sem("s_pad")
        s_spare = sem("s_spare")
        s_st1 = sem("s_st1")
        s_mv1 = sem("s_mv1")
        s_ve1 = sem("s_ve1")
        s_rstd1 = sem("s_rstd1")
        s_xn = sem("s_xn")
        s_xb = sem("s_xb")
        s_t1 = sem("s_t1")
        s_xch = sem("s_xch")
        s_xcl = sem("s_xcl")
        s_q = sem("s_q")
        s_kv = sem("s_kv")
        s_qb = sem("s_qb")
        s_kvb = sem("s_kvb")
        s_exp = sem("s_exp")
        s_qkp = sem("s_qkp")
        s_qkT = sem("s_qkT")
        s_qsel = sem("s_qsel")
        s_states = sem("s_states")
        s_sc = sem("s_sc")
        s_z = sem("s_z")
        s_state = sem("s_state")
        s_scores = sem("s_scores")
        s_zc = sem("s_zc")
        s_zinv = sem("s_zinv")
        s_zprod = sem("s_zprod")
        s_rz = sem("s_rz")
        s_o = sem("s_o")
        s_res0 = sem("s_res0")
        s_resT = sem("s_resT")
        s_res = sem("s_res")
        s_att = sem("s_att")
        s_attT = sem("s_attT")
        s_ath = sem("s_ath")
        s_atl = sem("s_atl")
        s_y = sem("s_y")
        s_x1s = sem("s_x1s")
        s_st2 = sem("s_st2")
        s_mv2 = sem("s_mv2")
        s_ve2 = sem("s_ve2")
        s_rstd2 = sem("s_rstd2")
        s_token = sem("s_token")
        s_x2n = sem("s_x2n")
        s_x2T = sem("s_x2T")
        s_x2f = sem("s_x2f")
        s_hid = sem("s_hid")
        s_hT = sem("s_hT")
        s_lgp = sem("s_lgp")
        s_pick = sem("s_pick")
        s_hot = sem("s_hot")
        s_ranked = sem("s_ranked")
        s_rank = sem("s_rank")
        s_place = sem("s_place")
        s_hots = sem("s_hots")
        s_count = sem("s_count")
        s_fill = sem("s_fill")
        s_rows2 = [sem(f"s_rows2_{r}") for r in range(RING)]
        s_outs = [sem(f"s_outs{r}") for r in range(RING)]
        s_x3n = sem("s_x3n")
        s_x3T = sem("s_x3T")
        s_x3h = sem("s_x3h")
        s_x3l = sem("s_x3l")
        s_prod = sem("s_prod")
        s_sums = sem("s_sums")
        s_tok2 = sem("s_tok2")

        block = stack.enter_context(nc.Block())

        def n(t, per=1, k=0):
            i, d = t
            return 2 * per * i + per * d + k

        def half(t):
            i, d = t
            return i + d // 2

        def slot(t):
            return t[1] % 2

        def schedule(eng, step):
            def one(i, u, live):
                step(*((i, u - k) if live(k) else None for k in range(STAGES)))
            lead = STAGES + STAGES % 2
            for j in range(lead):
                one(j // 2, j % 2, lambda k: j - k >= 0)
            with eng.Fori(lead // 2, TILES // 2, 1) as i:
                for u in range(2):
                    one(i, u, lambda k: True)
            for j in range(TILES, TILES + STAGES - 1):
                one(j // 2, j % 2, lambda k: j - k < TILES)

        def tile_no(t):
            return 2 * t[0] + t[1] if isinstance(t[0], int) else TILES

        def of(dram, t):
            return dram.rearrange("(i u) p n -> i u p n", u=2)[bass.ds(half(t), 1), slot(t), :, :]\
                .rearrange("o p n -> (o p) n")

        def m(t, per=1, k=0):
            i, d = t
            return RING * per * i + per * d + k

        def turn(t):
            i, d = t
            return i + d // RING

        def slot_schedule(eng, step):
            for j in range(RING):
                step(*((0, j - k) if j - k >= 0 else None for k in range(3)))
            with eng.Fori(1, SLOTS // RING, 1) as i:
                for u in range(RING):
                    step(*((i, u - k) for k in range(3)))
            for j in range(SLOTS, SLOTS + 2):
                step(*((j // RING, j % RING - k) if j - k < SLOTS else None for k in range(3)))

        def slot_no_of(t):
            return RING * t[0] + t[1] if isinstance(t[0], int) else SLOTS

        @block.sync
        def _(sp):
            for k, w in enumerate((wq, wk, wv, wo)):
                sp.dma_start(stage_small[:, :, k * D:(k + 1) * D],
                             w.rearrange("(k p) n -> p k n", p=P)).then_inc(s_wld, 16)
            sp.dma_start(w1_sb[:, :, :], w1.rearrange("(k p) n -> p k n", p=P)).then_inc(s_wld, 16)
            sp.dma_start(w2_sb[:, :], w2).then_inc(s_wld, 16)
            for k, b in enumerate((bq, bk, bv)):
                sp.dma_start(bias_qkv[:, k * D:(k + 1) * D],
                             b.rearrange("(o n) -> o n", o=1).to_broadcast((P, D))).then_inc(s_wld, 16)
            sp.dma_start(bias_o[:, :], bo.rearrange("(o n) -> o n", o=1).to_broadcast((P, D))).then_inc(s_wld, 16)
            sp.dma_start(bias_1[:, :], b1.rearrange("(n o) -> n o", o=1)).then_inc(s_wld, 16)
            sp.dma_start(bias_2[:, :], b2.rearrange("(o n) -> o n", o=1).to_broadcast((P, E))).then_inc(s_wld, 16)
            for e in range(E):
                sp.dma_start(stage_w[:, :, e, :], we[e, :, :].rearrange("(k p) n -> p k n", p=P)).then_inc(s_wld, 16)
            sp.dma_start(stage_be[:, :, :], be.rearrange("(o e) n -> o e n", o=1)).then_inc(s_wld, 16)
            sp.wait_ge(s_const, POOL_MADE)
            sp.dma_start(buckets[SPARE:SPARE + P, :], pad_row[:, :]).then_inc(s_spare, 16)

            def step(norm, project, attend, merge, route):
                if norm:
                    if tile_no(norm) >= 2:
                        sp.wait_ge(s_xb, n(norm, k=-1))
                        sp.wait_ge(s_xn, n(norm, k=-1))
                    sp.dma_start(x_in[:, slot(norm), :], of(x, norm)).then_inc(s_x[slot(norm)], 16)
                    if tile_no(norm) >= 2:
                        sp.wait_ge(s_t1, n(norm, k=-1))
                    sp.dma_start(ctx_in[:, slot(norm), :], of(ctx, norm)).then_inc(s_ctx[slot(norm)], 16)

            schedule(sp, step)

            for s in range(2):
                sp.wait_ge(s_bucket[s], 16 * (TILES // 2))
            sp.wait_ge(s_pad, 16 * E)
            sp.wait_ge(s_spare, 16)
            sp.wait_ge(s_fill, FILL_STEPS)

            def slot_step(load, transpose, multiply):
                if load:
                    r = load[1] % RING
                    first_row = sp.value_load(row_of[0:1, bass.ds(m(load), 1)], min_val=0, max_val=SPARE)
                    if slot_no_of(load) >= RING:
                        sp.wait_ge(s_outs[r], 16 * turn(load))
                    sp.dma_start(rows2[:, r, :], buckets[bass.ds(first_row, P), :]).then_inc(s_rows2[r], 16)

            slot_schedule(sp, slot_step)

        @block.gpsimd
        def _(pool):
            pool.memset(ident[:, :], 0.0).then_inc(s_const, 1)
            pool.memset(tri[:, :], 1.0).then_inc(s_const, 1)
            pool.memset(before[:, :], 1.0).then_inc(s_const, 1)
            pool.memset(ones[:, :], 1.0).then_inc(s_const, 1)
            pool.memset(neg_half[:, :], -0.5).then_inc(s_const, 1)
            pool.memset(eps_col[:, :], EPS).then_inc(s_const, 1)
            pool.memset(onehots[:, :], 0.0).then_inc(s_const, 1)
            pool.memset(pad_row[:, :], 0.0).then_inc(s_const, 1)
            pool.memset(zero_u[:, :], 0).then_inc(s_const, 1)
            pool.iota(iota8[:, :], pattern=[[1, E]], base=0, channel_multiplier=0,
                      allow_small_or_imprecise_dtypes=True).then_inc(s_const, 1)
            pool.iota(tokens[:, :], pattern=[[P, TILES]], base=0, channel_multiplier=1).then_inc(s_const, 1)
            pool.iota(pad_at[:, :], pattern=[[CAP, E]], base=0, channel_multiplier=1,
                      allow_small_or_imprecise_dtypes=True).then_inc(s_const, 1)
            pool.iota(multiples[:, :], pattern=[[P, TILES]], base=0, channel_multiplier=0,
                      allow_small_or_imprecise_dtypes=True).then_inc(s_const, 1)
            pool.iota(slot_no[:, :], pattern=[[1, SLOTS]], base=0, channel_multiplier=0,
                      allow_small_or_imprecise_dtypes=True).then_inc(s_const, 1)
            pool.wait_ge(s_const, 14)
            pool.affine_select(out=ident[:, :], in_=ident[:, :], compare_op=ALU.not_equal, fill=1.0,
                               base=0, pattern=[[-1, P]], channel_multiplier=1).then_inc(s_const, 1)
            pool.affine_select(out=tri[:, :], in_=tri[:, :], compare_op=ALU.is_ge, fill=0.0,
                               base=0, pattern=[[1, P]], channel_multiplier=-1).then_inc(s_const, 1)
            pool.affine_select(out=before[:, :], in_=before[:, :], compare_op=ALU.is_gt, fill=0.0,
                               base=0, pattern=[[1, P]], channel_multiplier=-1).then_inc(s_const, 1)
            pool.memset(pad_row[:, TOKEN:TOKEN + 1].bitcast(U32), NOBODY).then_inc(s_const, 1)
            pool.wait_ge(s_wld, WEIGHTS)

            def step(norm, project, attend, merge, route):
                if attend:
                    pool.wait_ge(s_zinv, n(attend, k=1))
                    pool.tensor_tensor(z_prod[:, :], z[:, :], z_inv[:, :], ALU.mult).then_inc(s_zprod, 1)
                if norm:
                    pool.wait_ge(s_mv1, n(norm, k=1))
                    pool.tensor_tensor(ve1[:, :], mv1[:, 1:2], eps_col[:, :], ALU.add).then_inc(s_ve1, 1)
                    pool.wait_ge(s_ve1, n(norm, k=1))
                    pool.tensor_tensor(rstd1[:, :], ve1[:, :], neg_half[:, :], ALU.pow).then_inc(s_rstd1, 1)
                if merge:
                    pool.wait_ge(s_mv2, n(merge, k=1))
                    pool.tensor_tensor(ve2[:, :], row[:, slot(merge), MEAN + 1:MEAN + 2], eps_col[:, :],
                                       ALU.add).then_inc(s_ve2, 1)
                    pool.wait_ge(s_ve2, n(merge, k=1))
                    pool.tensor_tensor(row[:, slot(merge), RSTD:RSTD + 1], ve2[:, :], neg_half[:, :],
                                       ALU.pow).then_inc(s_rstd2, 1)
                    pool.tensor_copy(row[:, slot(merge), TOKEN:TOKEN + 1].bitcast(U32),
                                     tokens[:, bass.ds(n(merge), 1)]).then_inc(s_token, 1)
                if project:
                    if tile_no(project) >= 2:
                        pool.wait_ge(s_x1s, n(project, k=-1))
                    pool.wait_ge(s_x[slot(project)], 16 * half(project) + 16)
                    pool.tensor_tensor(xb[:, slot(project), :], x_in[:, slot(project), :], bias_o[:, :],
                                       ALU.add).then_inc(s_xb, 1)
                if attend:
                    pool.wait_ge(s_res, n(attend, k=1))
                    pool.wait_ge(s_rz, n(attend, k=1))
                    pool.tensor_tensor(att[:, :], res[:, :], rz[:, :], ALU.mult).then_inc(s_att, 1)
                if route:
                    pool.wait_ge(s_place, n(route, k=1))
                    pool.wait_ge(s_token, n(route, k=1))
                    pool.tensor_tensor(onehots[:, :], onehots[:, :], onehot[:, :], ALU.add).then_inc(s_hots, 1)
                    pool.indirect_dma_start(buckets, bass.IndirectOffsetOnAxis(place[:, slot(route):slot(route) + 1], 0),
                                            row[:, slot(route), :], None).then_inc(s_bucket[slot(route)], 16)

            schedule(pool, step)

            pool.wait_ge(s_count, 3)
            for e in range(E):
                pool.indirect_dma_start(buckets, bass.IndirectOffsetOnAxis(pad_place[:, e:e + 1], 0),
                                        pad_row[:, :], None).then_inc(s_pad, 16)

            def slot_step(load, transpose, multiply):
                if multiply:
                    pool.wait_ge(s_sums, m(multiply, k=1))
                    pool.wait_ge(s_tok2, m(multiply, k=1))
                if load:
                    r = load[1] % RING
                    pool.wait_ge(s_rows2[r], 16 * turn(load) + 16)
                    pool.tensor_tensor(token[:, r:r + 1], rows2[:, r, TOKEN:TOKEN + 1].bitcast(U32), zero_u[:, :],
                                       ALU.add).then_inc(s_tok2, 1)
                if multiply:
                    r = multiply[1] % RING
                    pool.indirect_dma_start(out.rearrange("t p n -> (t p) n"),
                                            bass.IndirectOffsetOnAxis(token[:, r:r + 1], 0), sums[:, r, :], None,
                                            bounds_check=TOKENS - 1, oob_is_err=False).then_inc(s_outs[r], 16)

            slot_schedule(pool, slot_step)
            for r in range(RING):
                pool.wait_ge(s_outs[r], 16 * (SLOTS // RING))

        @block.scalar
        def _(act):
            act.wait_ge(s_wld, WEIGHTS)
            act.activation(wqkv_hi[:, :, :], stage_small[:, :, 0:3 * D], ACT.Copy).then_inc(s_hi, 1)
            act.activation(wo_hi[:, :, :], stage_small[:, :, 3 * D:4 * D], ACT.Copy).then_inc(s_hi, 1)
            act.activation(be_hi[:, :, :], stage_be[:, :, :], ACT.Copy).then_inc(s_hi, 1)
            for k in range(KC):
                act.activation(we_hi[:, k, :, :], stage_w[:, k, :, :], ACT.Copy).then_inc(s_hi, 1)
            act.wait_ge(s_const, POOL_MADE)
            act.activation(ones_row[:, :], tri[0:1, :], ACT.Copy).then_inc(s_hi, 1)
            act.wait_ge(s_cst, MADE)

            def step(norm, project, attend, merge, route):
                if route:
                    act.wait_ge(s_x2T, n(route, k=1))
                    act.activation(x2_f[:, :], b_z[:, 0:D], ACT.Copy).then_inc(s_x2f, 1)
                if attend:
                    act.wait_ge(s_states, n(attend, k=1))
                    act.activation(state[C:2 * C, :, :], b_st[C:2 * C, 0:D].rearrange("p (a b) -> p a b", b=C),
                                   ACT.Copy).then_inc(s_state, 1)
                    act.activation(state[2 * C:P, :, :], b_st[2 * C:P, 0:D].rearrange("p (a b) -> p a b", b=C),
                                   ACT.Copy).then_inc(s_state, 1)
                    act.wait_ge(s_z, n(attend, k=1))
                    act.activation(z[:, :], b_z[:, 0:D], ACT.Copy).then_inc(s_zc, 1)
                    act.activation(z_ln[:, :], b_z[:, 0:D], ACT.Ln).then_inc(s_zc, 1)
                    act.wait_ge(s_zc, n(attend, 2, 2))
                    act.activation(z_inv[:, :], z_ln[:, :], ACT.Exp, scale=-1.0).then_inc(s_zinv, 1)
                if route:
                    act.wait_ge(s_hid, n(route, k=1))
                    act.activation(hT[:, :], b_o[0:FF, 0:P], ACT.Relu, bias=bias_1[:, :]).then_inc(s_hT, 1)
                if merge:
                    act.wait_ge(s_attT, n(merge, k=1))
                    act.activation(attT_hi[:, :], b_sc[:, 0:D], ACT.Copy).then_inc(s_ath, 1)
                if project:
                    act.wait_ge(s_qb, n(project, k=1))
                    act.wait_ge(s_kvb, n(project, 2, 1))
                    act.activation(qk_exp[:, :], qk[:, :], ACT.Exp).then_inc(s_exp, 1)
                    act.activation(qk_pos[:, :], qk[:, :], ACT.Relu).then_inc(s_exp, 1)
                    act.wait_ge(s_qkT, n(project, k=1))
                    for h in range(2):
                        act.activation(qsel[:, slot(project), :, h, :], qkT[:, 0, :, :], ACT.Copy,
                                       scale=head_sel[:, h:h + 1]).then_inc(s_qsel, 1)
                if attend:
                    act.wait_ge(s_o, n(attend, k=1))
                    act.activation(res0[:, :, :],
                                   b_o[:, :].rearrange("p (a h b) -> p a h b", h=2, b=C)[:, :, 0, :],
                                   ACT.Copy, scale=head_sel[:, 0:1]).then_inc(s_res0, 1)
                if norm:
                    act.wait_ge(s_t1, n(norm, k=1))
                    act.activation(xc_hi[:, :], b_xc[:, :], ACT.Copy).then_inc(s_xch, 1)

            schedule(act, step)

            def slot_step(load, transpose, multiply):
                if transpose:
                    act.wait_ge(s_x3T, m(transpose, k=1))
                    act.activation(x3_hi[:, transpose[1] % 2, :], (b_xc, b_sc)[transpose[1] % 2][:, 0:D],
                                   ACT.Copy).then_inc(s_x3h, 1)

            slot_schedule(act, slot_step)

        @block.vector
        def _(dve):
            dve.memset(head_sel[:, 0:1], 0.0).then_inc(s_cst, 1)
            dve.memset(head_sel[:, 1:2], 1.0).then_inc(s_cst, 1)
            dve.memset(one_e[:, :], 1.0).then_inc(s_cst, 1)
            dve.wait_ge(s_cst, 3)
            for c in range(NCH):
                dve.memset(head_sel[C * c:C * c + HD, 0:1], 1.0)
                last = dve.memset(head_sel[C * c:C * c + HD, 1:2], 0.0)
            last.then_inc(s_cst, 1)
            dve.wait_ge(s_const, POOL_MADE)
            for c in range(NCH):
                for h in range(2 * PAIRS):
                    last = dve.tensor_copy(chunk_mask[C * c:C * c + C, h, :], tri[C * c:C * c + C, C * c:C * c + C])
            last.then_inc(s_cst, 1)
            dve.wait_ge(s_hi, KC + 4)
            dve.tensor_tensor(wqkv_lo[:, :, :], stage_small[:, :, 0:3 * D], wqkv_hi[:, :, :].bitcast(F32),
                              ALU.subtract).then_inc(s_cst, 1)
            dve.tensor_tensor(wo_lo[:, :, :], stage_small[:, :, 3 * D:4 * D], wo_hi[:, :, :].bitcast(F32),
                              ALU.subtract).then_inc(s_cst, 1)
            dve.tensor_tensor(be_lo[:, :, :], stage_be[:, :, :], be_hi[:, :, :].bitcast(F32), ALU.subtract).then_inc(s_cst, 1)
            for k in range(KC):
                dve.tensor_tensor(we_lo[:, k, :, :], stage_w[:, k, :, :], we_hi[:, k, :, :].bitcast(F32),
                                  ALU.subtract).then_inc(s_cst, 1)
            dve.wait_ge(s_cst, MADE)

            def step(norm, project, attend, merge, route):
                if project:
                    dve.wait_ge(s_xch, n(project, k=1))
                    dve.tensor_tensor(xc_lo[:, :], b_xc[:, :], xc_hi[:, :].bitcast(F32), ALU.subtract).then_inc(s_xcl, 1)
                if norm:
                    dve.wait_ge(s_x[slot(norm)], 16 * half(norm) + 16)
                    dve.bn_stats(st1[:, :], x_in[:, slot(norm), :]).then_inc(s_st1, 1)
                    dve.wait_ge(s_st1, n(norm, k=1))
                if attend:
                    dve.wait_ge(s_sc, n(attend, k=1))
                    dve.tensor_tensor(scores[:, :, :, :].rearrange("p a h b -> p (a h b)"), b_sc[:, :],
                                      chunk_mask[:, :, :].rearrange("p a b -> p (a b)"), ALU.mult).then_inc(s_scores, 1)
                if norm:
                    dve.bn_aggr(mv1[:, :], st1[:, :]).then_inc(s_mv1, 1)
                if merge:
                    dve.wait_ge(s_ath, n(merge, k=1))
                    dve.tensor_tensor(attT_lo[:, :], b_sc[:, 0:D], attT_hi[:, :].bitcast(F32), ALU.subtract).then_inc(s_atl, 1)
                if norm:
                    dve.wait_ge(s_rstd1, n(norm, k=1))
                    if tile_no(norm) >= 1:
                        dve.wait_ge(s_t1, n(norm))
                    dve.tensor_scalar(xn[:, :], x_in[:, slot(norm), :], mv1[:, 0:1], rstd1[:, 0:1],
                                      ALU.subtract, ALU.mult).then_inc(s_xn, 1)
                if attend:
                    dve.wait_ge(s_zprod, n(attend, k=1))
                    dve.scalar_tensor_tensor(rz[:, :], z_prod[:, :], 2.0, z_inv[:, :], ALU.subtract, ALU.mult,
                                             reverse0=True).then_inc(s_rz, 1)
                if project:
                    dve.wait_ge(s_q, n(project, k=1))
                    dve.tensor_tensor(qk[:, 0:D], b_q[:, 0:D], bias_qkv[:, 0:D], ALU.add).then_inc(s_qb, 1)
                    dve.wait_ge(s_kv, n(project, k=1))
                    dve.tensor_tensor(qk[:, D:2 * D], b_kv[:, 0:D], bias_qkv[:, D:2 * D], ALU.add).then_inc(s_kvb, 1)
                    dve.tensor_tensor(v[:, slot(project), :], b_kv[:, D:2 * D], bias_qkv[:, 2 * D:3 * D],
                                      ALU.add).then_inc(s_kvb, 1)
                if route:
                    dve.wait_ge(s_lgp, n(route, k=1))
                    dve.tensor_tensor(logits[:, :], b_xc[:, 0:E], bias_2[:, :], ALU.add).then_inc(s_pick, 1)
                    dve.wait_ge(s_pick, n(route, 3, 1))
                if merge:
                    dve.wait_ge(s_y, n(merge, k=1))
                    dve.wait_ge(s_xb, n(merge, k=1))
                    if tile_no(merge) >= 2:
                        dve.wait_ge(s_bucket[slot(merge)], 16 * half(merge))
                    dve.tensor_tensor(row[:, slot(merge), 0:D], b_st[:, 0:D], xb[:, slot(merge), :], ALU.add).then_inc(s_x1s, 1)
                if route:
                    dve.max(top[:, :], logits[:, :]).then_inc(s_pick, 1)
                    dve.wait_ge(s_pick, n(route, 3, 2))
                if merge:
                    dve.wait_ge(s_x1s, n(merge, k=1))
                    dve.bn_stats(st2[:, :], row[:, slot(merge), 0:D]).then_inc(s_st2, 1)
                if route:
                    dve.max_index(pick[:, :], top[:, :], logits[:, :]).then_inc(s_pick, 1)
                if merge:
                    dve.wait_ge(s_st2, n(merge, k=1))
                if project:
                    dve.wait_ge(s_exp, n(project, 2, 2))
                    dve.scalar_tensor_tensor(qkp[:, :], qk_exp[:, :], 1.0, qk_pos[:, :], ALU.min, ALU.add).then_inc(s_qkp, 1)
                if merge:
                    dve.bn_aggr(row[:, slot(merge), MEAN:MEAN + 2], st2[:, :]).then_inc(s_mv2, 1)
                if route:
                    if tile_no(route) >= 1:
                        dve.wait_ge(s_hots, n(route))
                    dve.wait_ge(s_pick, n(route, 3, 3))
                    dve.tensor_scalar(onehot[:, :], iota8[:, :], pick[:, 0:1], None, ALU.is_equal).then_inc(s_hot, 1)
                if project:
                    dve.wait_ge(s_qkp, n(project, k=1))
                    dve.transpose(qkT[:, :, :, :].rearrange("p q a b -> p (q a b)"), qkp[:, :]).then_inc(s_qkT, 1)
                if merge:
                    dve.wait_ge(s_rstd2, n(merge, k=1))
                    dve.tensor_scalar(x2n[:, :], row[:, slot(merge), 0:D], row[:, slot(merge), MEAN:MEAN + 1],
                                      row[:, slot(merge), RSTD:RSTD + 1], ALU.subtract, ALU.mult).then_inc(s_x2n, 1)
                if attend:
                    dve.wait_ge(s_res0, n(attend, k=1))
                    dve.scalar_tensor_tensor(resT[:, :, :],
                                             b_o[:, :].rearrange("p (a h b) -> p a h b", h=2, b=C)[:, :, 1, :],
                                             head_sel[:, 1:2], res0[:, :, :], ALU.mult, ALU.add).then_inc(s_resT, 1)
                    dve.wait_ge(s_resT, n(attend, k=1))
                    dve.transpose(res[:, :], resT[:, :, :].rearrange("p a b -> p (a b)")).then_inc(s_res, 1)
                if route:
                    dve.wait_ge(s_ranked, n(route, k=1))
                    dve.scalar_tensor_tensor(ranked[:, :], b_q[:, D:D + E], 1.0, onehot[:, :], ALU.mult, ALU.mult,
                                             accum_out=rank[:, :]).then_inc(s_rank, 1)
                    dve.wait_ge(s_rank, n(route, k=1))
                    dve.tensor_scalar(place[:, slot(route):slot(route) + 1], pick[:, 0:1], float(CAP), rank[:, 0:1],
                                      ALU.mult, ALU.add).then_inc(s_place, 1)

            schedule(dve, step)

            done = [0]

            def chain(ins):
                done[0] += 1
                ins.then_inc(s_fill, 1)
                dve.wait_ge(s_fill, done[0])

            dve.wait_ge(s_count, 1)
            dve.tensor_copy(count[:, :], b_q[:, 0:E]).then_inc(s_count, 1)
            dve.wait_ge(s_count, 2)
            dve.tensor_tensor(pad_place[:, :], count[:, :], pad_at[:, :], ALU.add).then_inc(s_count, 1)
            for e in range(E):
                chain(dve.tensor_scalar(over[:, :], multiples[:, :], count[0:1, e:e + 1], None, ALU.is_lt, ALU.add,
                                        accum_out=fill[:, e:e + 1]))
            chain(dve.tensor_tensor_scan(fill_sum[:, :], one_e[:, :], fill[:, :], 0.0, ALU.mult, ALU.add))
            chain(dve.tensor_scalar(jump[:, :], fill[:, :], float(-P), float(CAP), ALU.mult, ALU.add))
            chain(dve.tensor_scalar(slot_row[:, :], slot_no[:, :], float(P), None, ALU.mult))
            chain(dve.memset(slot_e[:, :], 0.0))
            for e in range(E - 1):
                chain(dve.tensor_scalar(step_row[:, :], slot_no[:, :], fill_sum[:, e:e + 1], jump[:, e:e + 1],
                                        ALU.is_ge, ALU.mult))
                chain(dve.tensor_tensor(slot_row[:, :], slot_row[:, :], step_row[:, :], ALU.add))
                chain(dve.scalar_tensor_tensor(slot_e[:, :], slot_no[:, :], fill_sum[:, e:e + 1], slot_e[:, :],
                                               ALU.is_ge, ALU.add))
            chain(dve.tensor_scalar(slot_used[:, :], slot_no[:, :], fill_sum[:, E - 1:E], None, ALU.is_lt))
            chain(dve.scalar_tensor_tensor(slot_row[:, :], slot_row[:, :], float(SPARE), slot_used[:, :],
                                           ALU.subtract, ALU.mult))
            chain(dve.tensor_scalar(row_of[:, :], slot_row[:, :], float(SPARE), None, ALU.add))
            chain(dve.tensor_copy(expert_of[:, :], slot_e[:, :]))
            assert done[0] == FILL_STEPS

            def slot_step(load, transpose, multiply):
                if load:
                    r = load[1] % RING
                    dve.wait_ge(s_rows2[r], 16 * turn(load) + 16)
                    if slot_no_of(load) >= 2:
                        dve.wait_ge(s_x3T, m(load, k=-1))
                    dve.tensor_scalar(x3n[:, load[1] % 2, :], rows2[:, r, 0:D], rows2[:, r, MEAN:MEAN + 1],
                                      rows2[:, r, RSTD:RSTD + 1], ALU.subtract, ALU.mult).then_inc(s_x3n, 1)
                if transpose:
                    dve.wait_ge(s_x3h, m(transpose, k=1))
                    dve.tensor_tensor(x3_lo[:, transpose[1] % 2, :], (b_xc, b_sc)[transpose[1] % 2][:, 0:D],
                                      x3_hi[:, transpose[1] % 2, :].bitcast(F32), ALU.subtract).then_inc(s_x3l, 1)
                if multiply:
                    r = multiply[1] % RING
                    dve.wait_ge(s_prod, m(multiply, k=1))
                    if slot_no_of(multiply) >= RING:
                        dve.wait_ge(s_outs[r], 16 * turn(multiply))
                    dve.tensor_tensor(sums[:, r, :], (b_q, b_kv)[multiply[1] % 2][:, 0:D], rows2[:, r, 0:D],
                                      ALU.add).then_inc(s_sums, 1)

            slot_schedule(dve, slot_step)

        @block.tensor
        def _(pe):
            pe.wait_ge(s_const, POOL_MADE)
            pe.wait_ge(s_cst, MADE)
            pe.wait_ge(s_wld, WEIGHTS)

            def split_product(dst, lhs_hi, lhs_lo, rhs_hi, rhs_lo, last_of_group=True):
                parts = [(k, a, b) for k in range(KC) for a, b in
                         ((lhs_hi, rhs_hi), (lhs_hi, rhs_lo), (lhs_lo, rhs_hi))]
                for i, (k, a, b) in enumerate(parts):
                    last = pe.matmul(dst, a(k), b(k), start=(i == 0), stop=(last_of_group and i == len(parts) - 1))
                return last

            def rows(c):
                return slice(C * c, C * c + C)

            def step(norm, project, attend, merge, route):
                if attend:
                    a = slot(attend)
                    pe.wait_ge(s_cst, MADE)
                    pe.wait_ge(s_qsel, n(attend, 2, 2))
                    pe.wait_ge(s_kvb, n(attend, 2, 2))
                    if tile_no(attend) >= 2:
                        pe.wait_ge(s_x1s, n(attend, k=-1))
                        pe.wait_ge(s_atl, n(attend, k=-1))
                    for p in range(PAIRS):
                        for c in range(NCH - 1, 0, -1):
                            last = pe.matmul(b_st[rows(c), C * p:C * p + C], qkp[0:C * c, D + C * p:D + C * p + C],
                                             v[0:C * c, a, C * p:C * p + C], start=True, stop=True)
                    last.then_inc(s_states, 1)
                    for p in range(PAIRS):
                        for c in range(NCH):
                            last = pe.matmul(b_sc[rows(c), 2 * C * p:2 * C * (p + 1)], qkT[rows(c), 1, p, :],
                                             qsel[rows(c), a, p, :, :], start=True, stop=True)
                    last.then_inc(s_sc, 1)
                    if tile_no(attend) >= 2:
                        pe.wait_ge(s_x2f, n(attend, k=-1))
                    pe.matmul(b_z[:, 0:D], tri[:, :], qkp[:, 0:D], start=True, stop=True).then_inc(s_z, 1)
                if route:
                    pe.wait_ge(s_x2f, n(route, k=1))
                    pe.wait_ge(s_resT, n(route, k=2 if merge else 1))
                    for k in range(KC):
                        last = pe.matmul(b_o[0:FF, 0:P], w1_sb[:, k, :], x2_f[:, k * P:(k + 1) * P],
                                         start=(k == 0), stop=(k == KC - 1))
                    last.then_inc(s_hid, 1)
                if merge:
                    pe.wait_ge(s_att, n(merge, k=1))
                    if attend:
                        pe.wait_ge(s_scores, n(attend, k=1))
                    for k in range(KC):
                        last = pe.transpose(b_sc[:, k * P:(k + 1) * P], att[:, k * P:(k + 1) * P], ident[:, :])
                    last.then_inc(s_attT, 1)
                if project:
                    pe.wait_ge(s_xcl, n(project, k=1))
                    if tile_no(project) >= 4:
                        pe.wait_ge(s_rank, n(project, k=-3))
                    split_product(b_q[:, 0:D],
                                  lambda k: xc_hi[:, k * P:(k + 1) * P], lambda k: xc_lo[:, k * P:(k + 1) * P],
                                  lambda k: wqkv_hi[:, k, 0:D], lambda k: wqkv_lo[:, k, 0:D]).then_inc(s_q, 1)
                    if tile_no(project) >= 1:
                        pe.wait_ge(s_kvb, n(project, 2))
                    split_product(b_kv[:, :],
                                  lambda k: xc_hi[:, D + k * P:D + (k + 1) * P], lambda k: xc_lo[:, D + k * P:D + (k + 1) * P],
                                  lambda k: wqkv_hi[:, k, D:3 * D], lambda k: wqkv_lo[:, k, D:3 * D]).then_inc(s_kv, 1)
                if route:
                    pe.wait_ge(s_hT, n(route, k=1))
                    pe.matmul(b_xc[:, 0:E], hT[:, :], w2_sb[:, :], start=True, stop=True).then_inc(s_lgp, 1)
                if merge:
                    pe.wait_ge(s_atl, n(merge, k=1))
                    if attend:
                        pe.wait_ge(s_state, n(attend, 2, 2))
                    split_product(b_st[:, 0:D],
                                  lambda k: attT_hi[:, k * P:(k + 1) * P], lambda k: attT_lo[:, k * P:(k + 1) * P],
                                  lambda k: wo_hi[:, k, :], lambda k: wo_lo[:, k, :]).then_inc(s_y, 1)
                if attend:
                    pe.wait_ge(s_cst, MADE)
                    pe.wait_ge(s_state, n(attend, 2, 2))
                    pe.wait_ge(s_scores, n(attend, k=1))
                    if merge:
                        pe.wait_ge(s_resT, n(attend))
                    for p in range(PAIRS):
                        for c in range(NCH):
                            last = pe.matmul(b_o[rows(c), 2 * C * p:2 * C * (p + 1)], v[rows(c), a, C * p:C * p + C],
                                             scores[rows(c), p, :, :], start=True, stop=(c == 0))
                        for c in range(1, NCH):
                            last = pe.matmul(b_o[rows(c), 2 * C * p:2 * C * (p + 1)], state[rows(c), p, :],
                                             qsel[rows(c), a, p, :, :], start=False, stop=True)
                    last.then_inc(s_o, 1)
                if norm:
                    pe.wait_ge(s_xn, n(norm, k=1))
                    pe.wait_ge(s_ctx[slot(norm)], 16 * half(norm) + 16)
                    if project:
                        pe.wait_ge(s_xcl, n(norm))
                    if route:
                        pe.wait_ge(s_pick, n(route, 3, 1))
                    for k in range(KC):
                        pe.transpose(b_xc[:, k * P:(k + 1) * P], xn[:, k * P:(k + 1) * P], ident[:, :])
                    for k in range(KC):
                        last = pe.transpose(b_xc[:, D + k * P:D + (k + 1) * P],
                                            ctx_in[:, slot(norm), k * P:(k + 1) * P], ident[:, :])
                    last.then_inc(s_t1, 1)
                if route:
                    pe.wait_ge(s_hot, n(route, k=1))
                    if project:
                        pe.wait_ge(s_qb, n(project, k=1))
                    if tile_no(route) >= 1:
                        pe.wait_ge(s_hots, n(route))
                    pe.matmul(b_q[:, D:D + E], before[:, :], onehot[:, :], start=True, stop=False)
                    pe.matmul(b_q[:, D:D + E], ones[:, :], onehots[:, :], start=False, stop=True).then_inc(s_ranked, 1)
                if merge:
                    pe.wait_ge(s_x2n, n(merge, k=1))
                    if attend:
                        pe.wait_ge(s_zc, n(attend, 2, 2))
                    for k in range(KC):
                        last = pe.transpose(b_z[:, k * P:(k + 1) * P], x2n[:, k * P:(k + 1) * P], ident[:, :])
                    last.then_inc(s_x2T, 1)

            schedule(pe, step)
            pe.wait_ge(s_hots, TILES)
            pe.wait_ge(s_rank, TILES)
            pe.matmul(b_q[:, 0:E], ones[:, :], onehots[:, :], start=True, stop=True).then_inc(s_count, 1)
            pe.wait_ge(s_fill, FILL_STEPS)

            def slot_step(load, transpose, multiply):
                if transpose:
                    h = transpose[1] % 2
                    pe.wait_ge(s_x3n, m(transpose, k=1))
                    if slot_no_of(transpose) >= 2:
                        pe.wait_ge(s_x3l, m(transpose, k=-1))
                    for k in range(KC):
                        last = pe.transpose((b_xc, b_sc)[h][:, k * P:(k + 1) * P], x3n[:, h, k * P:(k + 1) * P], ident[:, :])
                    last.then_inc(s_x3T, 1)
                if multiply:
                    h = multiply[1] % 2
                    e = pe.value_load(expert_of[0:1, bass.ds(m(multiply), 1)], min_val=0, max_val=E - 1)
                    pe.wait_ge(s_x3l, m(multiply, k=1))
                    if slot_no_of(multiply) >= 2:
                        pe.wait_ge(s_sums, m(multiply, k=-1))
                    dst = (b_q, b_kv)[h][:, 0:D]
                    split_product(dst,
                                  lambda k: x3_hi[:, h, k * P:(k + 1) * P], lambda k: x3_lo[:, h, k * P:(k + 1) * P],
                                  lambda k: we_hi[:, k, bass.ds(e, 1), :], lambda k: we_lo[:, k, bass.ds(e, 1), :],
                                  last_of_group=False)
                    pe.matmul(dst, ones_row[:, :], be_hi[0:1, bass.ds(e, 1), :], start=False, stop=False)
                    pe.matmul(dst, ones_row[:, :], be_lo[0:1, bass.ds(e, 1), :], start=False, stop=True)\
                        .then_inc(s_prod, 1)

            slot_schedule(pe, slot_step)


_INS = ["x", "ctx_1024", "L0_xattn_Wq", "L0_xattn_bq", "L0_xattn_Wk", "L0_xattn_bk", "L0_xattn_Wv",
        "L0_xattn_bv", "L0_xattn_Wo", "L0_xattn_bo", "L0_ffn_W1", "L0_ffn_b1", "L0_ffn_W2", "L0_ffn_b2",
        "L0_ffn_expert_W", "L0_ffn_expert_b"]


def kernel(**inputs):
    import numpy as np
    import concourse.bacc as bacc
    from concourse.bass_utils import run_bass_kernel_spmd

    nc = bacc.Bacc("TRN2", target_bir_lowering=False, num_devices=1)
    arrays, args = {}, []
    for name in _INS:
        a = np.ascontiguousarray(inputs[name])
        arrays[f"in_{name}"] = a
        args.append(nc.dram_tensor(f"in_{name}", a.shape, mybir.dt.from_np(a.dtype), kind="ExternalInput").ap())
    out = nc.dram_tensor("out", arrays["in_x"].shape, F32, kind="ExternalOutput").ap()
    build(nc, *args, out)
    return run_bass_kernel_spmd(nc, [arrays], core_ids=[0]).results[0]["out"]
```

```python
import concourse.bass as bass
from concourse import mybir
from contextlib import ExitStack

F32 = mybir.dt.float32
F32R = mybir.dt.float32r
BF16 = mybir.dt.bfloat16
U32 = mybir.dt.uint32
I32 = mybir.dt.int32
ALU = mybir.AluOpType
ACT = mybir.ActivationFunctionType


def build(nc, x, ctx, wq, bq, wk, bk, wv, bv, wo, bo, w1, b1, w2, b2, we, be, out):
    TILES, P, D = x.shape
    KC = D // P
    E = we.shape[0]
    FF = w1.shape[1]
    C = 32
    NCH = P // C
    PAIRS = D // C
    HD = C // 2
    EPS = 1e-5
    TOKENS = TILES * P
    CAP = TOKENS + P
    SPARE = E * CAP
    ROW = D + 4
    MEAN, RSTD, TOKEN = D, D + 2, D + 3
    NOBODY = 1 << 20
    SLOTS = TILES + E
    STAGES = 5
    RING = 8
    WEIGHTS = 16 * 12
    EXPERTS = 16 * (E + 1)
    POOL_MADE = 18
    MADE = 7
    FILL_STEPS = E + 4 + 3 * (E - 1) + 5

    with ExitStack() as stack:
        def sb(name, shape, dt=F32):
            return stack.enter_context(nc.sbuf_tensor(name, shape, dt))

        def bank(name):
            return stack.enter_context(nc.psum_tensor(name, [P, 512], F32))

        def sem(name):
            return stack.enter_context(nc.semaphore(name))

        buckets = nc.dram_tensor("buckets", (SPARE + P, ROW), F32, kind="Internal").ap()

        row_of = sb("row_of", [1, SLOTS], I32)
        expert_of = sb("expert_of", [1, SLOTS + 4], I32)

        ident = sb("ident", [P, P])
        tri = sb("tri", [P, P])
        before = sb("before", [P, P], BF16)
        ones = sb("ones", [P, P], BF16)
        chunk_mask = sb("chunk_mask", [P, 2 * PAIRS, C])
        head_sel = sb("head_sel", [P, 2])
        neg_half = sb("neg_half", [P, 1])
        eps_col = sb("eps_col", [P, 1])
        iota8 = sb("iota8", [P, E])
        tokens = sb("tokens", [P, TILES], U32)
        pad_row = sb("pad_row", [P, ROW])
        pad_at = sb("pad_at", [P, E])
        multiples = sb("multiples", [1, TILES])
        slot_no = sb("slot_no", [1, SLOTS])
        zero_u = sb("zero_u", [P, 1], U32)
        bias_qkv = sb("bias_qkv", [P, 3 * D])
        bias_o = sb("bias_o", [P, D])
        bias_1 = sb("bias_1", [FF, 1])
        bias_2 = sb("bias_2", [P, E])
        stage_w = sb("stage_w", [P, KC, E, D])
        wqkv_hi = sb("wqkv_hi", [P, KC, 3 * D], F32R)
        wqkv_lo = sb("wqkv_lo", [P, KC, 3 * D], F32R)
        wo_hi = sb("wo_hi", [P, KC, D], F32R)
        wo_lo = sb("wo_lo", [P, KC, D], F32R)
        we_hi = sb("we_hi", [P, KC, E, D], F32R)
        we_lo = sb("we_lo", [P, KC, E, D], F32R)
        be_hi = sb("be_hi", [1, E, D], F32R)
        be_lo = sb("be_lo", [1, E, D], F32R)
        stage_be = sb("stage_be", [1, E, D])
        ones_row = sb("ones_row", [1, P], F32R)
        stage_small = sb("stage_small", [P, KC, 4 * D])
        w1_sb = sb("w1_sb", [P, KC, FF])
        w2_sb = sb("w2_sb", [FF, E])
        x_in = sb("x_in", [P, 2, D])
        ctx_in = sb("ctx_in", [P, 2, D])
        st1 = sb("st1", [P, 6])
        mv1 = sb("mv1", [P, 2])
        ve1 = sb("ve1", [P, 1])
        rstd1 = sb("rstd1", [P, 1])
        xn = sb("xn", [P, D])
        xc_hi = sb("xc_hi", [P, 2 * D], F32R)
        xc_lo = sb("xc_lo", [P, 2 * D], F32R)
        qk = sb("qk", [P, 2 * D])
        v = sb("v", [P, 2, D])
        qk_exp = sb("qk_exp", [P, 2 * D])
        qk_pos = sb("qk_pos", [P, 2 * D])
        qkp = sb("qkp", [P, 2 * D])
        qkT = sb("qkT", [P, 2, PAIRS, C])
        qsel = sb("qsel", [P, 2, PAIRS, 2, C])
        state = sb("state", [P, PAIRS, C])
        scores = sb("scores", [P, PAIRS, 2, C])
        z = sb("z", [P, D])
        z_ln = sb("z_ln", [P, D])
        z_inv = sb("z_inv", [P, D])
        z_prod = sb("z_prod", [P, D])
        rz = sb("rz", [P, D])
        res0 = sb("res0", [P, PAIRS, C])
        resT = sb("resT", [P, PAIRS, C])
        res = sb("res", [P, D])
        att = sb("att", [P, D])
        attT_hi = sb("attT_hi", [P, D], F32R)
        attT_lo = sb("attT_lo", [P, D], F32R)
        xb = sb("xb", [P, 2, D])
        row = sb("row", [P, 2, ROW])
        st2 = sb("st2", [P, 6])
        ve2 = sb("ve2", [P, 1])
        x2n = sb("x2n", [P, D])
        x2_f = sb("x2_f", [P, D])
        hT = sb("hT", [FF, P])
        logits = sb("logits", [P, E])
        top = sb("top", [P, 8])
        pick = sb("pick", [P, 8], U32)
        onehot = sb("onehot", [P, E], BF16)
        onehots = sb("onehots", [P, E], BF16)
        ranked = sb("ranked", [P, E])
        rank = sb("rank", [P, 1])
        place = sb("place", [P, 2], U32)
        count = sb("count", [P, E])
        pad_place = sb("pad_place", [P, E], U32)
        over = sb("over", [1, TILES])
        fill = sb("fill", [1, E])
        fill_sum = sb("fill_sum", [1, E])
        one_e = sb("one_e", [1, E])
        jump = sb("jump", [1, E])
        step_row = sb("step_row", [1, SLOTS])
        slot_e = sb("slot_e", [1, SLOTS])
        slot_row = sb("slot_row", [1, SLOTS])
        slot_used = sb("slot_used", [1, SLOTS])
        rows2 = sb("rows2", [P, RING, ROW])
        x3n = sb("x3n", [P, 2, D])
        x3_hi = sb("x3_hi", [P, 2, D], F32R)
        x3_lo = sb("x3_lo", [P, 2, D], F32R)
        sums = sb("sums", [P, RING, D])
        token = sb("token", [P, RING], U32)

        b_xc = bank("b_xc")
        b_qk = bank("b_qk")
        b_v = bank("b_v")
        b_sc = bank("b_sc")
        b_st = bank("b_st")
        b_y = bank("b_y")
        b_z = bank("b_z")
        b_o = bank("b_o")

        s_wld = sem("s_wld")
        s_eld = sem("s_eld")
        s_ehi = sem("s_ehi")
        s_elo = sem("s_elo")
        s_cst = sem("s_cst")
        s_hi = sem("s_hi")
        s_const = sem("s_const")
        s_x = [sem("s_x0"), sem("s_x1")]
        s_ctx = [sem("s_ctx0"), sem("s_ctx1")]
        s_bucket = [sem("s_bucket0"), sem("s_bucket1")]
        s_pad = sem("s_pad")
        s_spare = sem("s_spare")
        s_st1 = sem("s_st1")
        s_mv1 = sem("s_mv1")
        s_ve1 = sem("s_ve1")
        s_rstd1 = sem("s_rstd1")
        s_xn = sem("s_xn")
        s_xb = sem("s_xb")
        s_t1 = sem("s_t1")
        s_xch = sem("s_xch")
        s_xcl = sem("s_xcl")
        s_qk = sem("s_qk")
        s_v = sem("s_v")
        s_qkb = sem("s_qkb")
        s_vb = sem("s_vb")
        s_exp = sem("s_exp")
        s_qkp = sem("s_qkp")
        s_qkT = sem("s_qkT")
        s_qsel = sem("s_qsel")
        s_states = sem("s_states")
        s_sc = sem("s_sc")
        s_z = sem("s_z")
        s_state = sem("s_state")
        s_scores = sem("s_scores")
        s_zc = sem("s_zc")
        s_zinv = sem("s_zinv")
        s_zprod = sem("s_zprod")
        s_rz = sem("s_rz")
        s_o = sem("s_o")
        s_res0 = sem("s_res0")
        s_resT = sem("s_resT")
        s_res = sem("s_res")
        s_att = sem("s_att")
        s_attT = sem("s_attT")
        s_ath = sem("s_ath")
        s_atl = sem("s_atl")
        s_y = sem("s_y")
        s_x1s = sem("s_x1s")
        s_st2 = sem("s_st2")
        s_mv2 = sem("s_mv2")
        s_ve2 = sem("s_ve2")
        s_rstd2 = sem("s_rstd2")
        s_token = sem("s_token")
        s_x2n = sem("s_x2n")
        s_x2T = sem("s_x2T")
        s_x2f = sem("s_x2f")
        s_hid = sem("s_hid")
        s_hT = sem("s_hT")
        s_lgp = sem("s_lgp")
        s_pick = sem("s_pick")
        s_hot = sem("s_hot")
        s_ranked = sem("s_ranked")
        s_rank = sem("s_rank")
        s_place = sem("s_place")
        s_hots = sem("s_hots")
        s_count = sem("s_count")
        s_fill = sem("s_fill")
        s_rows2 = [sem(f"s_rows2_{r}") for r in range(RING)]
        s_outs = [sem(f"s_outs{r}") for r in range(RING)]
        s_x3n = sem("s_x3n")
        s_x3T = sem("s_x3T")
        s_x3h = sem("s_x3h")
        s_x3l = sem("s_x3l")
        s_prod = sem("s_prod")
        s_sums = sem("s_sums")
        s_tok2 = sem("s_tok2")

        block = stack.enter_context(nc.Block())

        def n(t, per=1, k=0):
            i, d = t
            return 2 * per * i + per * d + k

        def half(t):
            i, d = t
            return i + d // 2

        def slot(t):
            return t[1] % 2

        def schedule(eng, step):
            def one(i, u, live):
                step(*((i, u - k) if live(k) else None for k in range(STAGES)))
            lead = STAGES + STAGES % 2
            for j in range(lead):
                one(j // 2, j % 2, lambda k: j - k >= 0)
            with eng.Fori(lead // 2, TILES // 2, 1) as i:
                for u in range(2):
                    one(i, u, lambda k: True)
            for j in range(TILES, TILES + STAGES - 1):
                one(j // 2, j % 2, lambda k: j - k < TILES)

        def tile_no(t):
            return 2 * t[0] + t[1] if isinstance(t[0], int) else TILES

        def of(dram, t):
            return dram.rearrange("(i u) p n -> i u p n", u=2)[bass.ds(half(t), 1), slot(t), :, :]\
                .rearrange("o p n -> (o p) n")

        def m(t, per=1, k=0):
            i, d = t
            return RING * per * i + per * d + k

        def turn(t):
            i, d = t
            return i + d // RING

        def slot_schedule(eng, step, begin=lambda first, how_many: None):
            begin((0, -2), RING)
            for j in range(RING):
                step(*((0, j - k) if j - k >= 0 else None for k in range(3)))
            with eng.Fori(1, SLOTS // RING, 1) as i:
                begin((i, -2), RING)
                for u in range(RING):
                    step(*((i, u - k) for k in range(3)))
            begin((SLOTS // RING, -2), 2)
            for j in range(SLOTS, SLOTS + 2):
                step(*((j // RING, j % RING - k) if j - k < SLOTS else None for k in range(3)))

        def slot_no_of(t):
            return RING * t[0] + t[1] if isinstance(t[0], int) else SLOTS

        @block.sync
        def _(sp):
            for k, w in enumerate((wq, wk, wv, wo)):
                sp.dma_start(stage_small[:, :, k * D:(k + 1) * D],
                             w.rearrange("(k p) n -> p k n", p=P)).then_inc(s_wld, 16)
            sp.dma_start(w1_sb[:, :, :], w1.rearrange("(k p) n -> p k n", p=P)).then_inc(s_wld, 16)
            sp.dma_start(w2_sb[:, :], w2).then_inc(s_wld, 16)
            for k, b in enumerate((bq, bk, bv)):
                sp.dma_start(bias_qkv[:, k * D:(k + 1) * D],
                             b.rearrange("(o n) -> o n", o=1).to_broadcast((P, D))).then_inc(s_wld, 16)
            sp.dma_start(bias_o[:, :], bo.rearrange("(o n) -> o n", o=1).to_broadcast((P, D))).then_inc(s_wld, 16)
            sp.dma_start(bias_1[:, :], b1.rearrange("(n o) -> n o", o=1)).then_inc(s_wld, 16)
            sp.dma_start(bias_2[:, :], b2.rearrange("(o n) -> o n", o=1).to_broadcast((P, E))).then_inc(s_wld, 16)

            def load_experts():
                for e in range(E):
                    sp.dma_start(stage_w[:, :, e, :], we[e, :, :].rearrange("(k p) n -> p k n", p=P)).then_inc(s_eld, 16)
                sp.dma_start(stage_be[:, :, :], be.rearrange("(o e) n -> o e n", o=1)).then_inc(s_eld, 16)
                sp.wait_ge(s_const, POOL_MADE)
                sp.dma_start(buckets[SPARE:SPARE + P, :], pad_row[:, :]).then_inc(s_spare, 16)

            def step(norm, project, attend, merge, route):
                if norm:
                    if tile_no(norm) >= 2:
                        sp.wait_ge(s_xb, n(norm, k=-1))
                        sp.wait_ge(s_xn, n(norm, k=-1))
                    sp.dma_start(x_in[:, slot(norm), :], of(x, norm)).then_inc(s_x[slot(norm)], 16)
                    if tile_no(norm) >= 2:
                        sp.wait_ge(s_t1, n(norm, k=-1))
                    sp.dma_start(ctx_in[:, slot(norm), :], of(ctx, norm)).then_inc(s_ctx[slot(norm)], 16)
                    if tile_no(norm) == 1:
                        load_experts()

            schedule(sp, step)

            for s in range(2):
                sp.wait_ge(s_bucket[s], 16 * (TILES // 2))
            sp.wait_ge(s_pad, 16 * E)
            sp.wait_ge(s_spare, 16)
            sp.wait_ge(s_fill, FILL_STEPS)

            first_rows = []

            def load_rows(first, how_many):
                if how_many == RING:
                    first_rows.extend(nc.values_load_multi_w_load_instructions(
                        row_of[0:1, bass.ds(m(first, k=2), how_many)], [mybir.EngineType.SP], min_val=0, max_val=SPARE,
                        skip_runtime_bounds_check_because="the tables are computed on the chip within these bounds")[1])

            def slot_step(load, transpose, multiply):
                if load:
                    r = load[1] % RING
                    first_row = first_rows.pop(0)
                    if slot_no_of(load) >= RING:
                        sp.wait_ge(s_sums, m(load, k=1 - RING))
                        sp.wait_ge(s_tok2, m(load, k=1 - RING))
                    sp.dma_start(rows2[:, r, :], buckets[bass.ds(first_row, P), :]).then_inc(s_rows2[r], 16)

            slot_schedule(sp, slot_step, load_rows)

        @block.gpsimd
        def _(pool):
            pool.memset(ident[:, :], 0.0).then_inc(s_const, 1)
            pool.memset(tri[:, :], 1.0).then_inc(s_const, 1)
            pool.memset(before[:, :], 1.0).then_inc(s_const, 1)
            pool.memset(ones[:, :], 1.0).then_inc(s_const, 1)
            pool.memset(neg_half[:, :], -0.5).then_inc(s_const, 1)
            pool.memset(eps_col[:, :], EPS).then_inc(s_const, 1)
            pool.memset(onehots[:, :], 0.0).then_inc(s_const, 1)
            pool.memset(pad_row[:, :], 0.0).then_inc(s_const, 1)
            pool.memset(zero_u[:, :], 0).then_inc(s_const, 1)
            pool.iota(iota8[:, :], pattern=[[1, E]], base=0, channel_multiplier=0,
                      allow_small_or_imprecise_dtypes=True).then_inc(s_const, 1)
            pool.iota(tokens[:, :], pattern=[[P, TILES]], base=0, channel_multiplier=1).then_inc(s_const, 1)
            pool.iota(pad_at[:, :], pattern=[[CAP, E]], base=0, channel_multiplier=1,
                      allow_small_or_imprecise_dtypes=True).then_inc(s_const, 1)
            pool.iota(multiples[:, :], pattern=[[P, TILES]], base=0, channel_multiplier=0,
                      allow_small_or_imprecise_dtypes=True).then_inc(s_const, 1)
            pool.iota(slot_no[:, :], pattern=[[1, SLOTS]], base=0, channel_multiplier=0,
                      allow_small_or_imprecise_dtypes=True).then_inc(s_const, 1)
            pool.wait_ge(s_const, 14)
            pool.affine_select(out=ident[:, :], in_=ident[:, :], compare_op=ALU.not_equal, fill=1.0,
                               base=0, pattern=[[-1, P]], channel_multiplier=1).then_inc(s_const, 1)
            pool.affine_select(out=tri[:, :], in_=tri[:, :], compare_op=ALU.is_ge, fill=0.0,
                               base=0, pattern=[[1, P]], channel_multiplier=-1).then_inc(s_const, 1)
            pool.affine_select(out=before[:, :], in_=before[:, :], compare_op=ALU.is_gt, fill=0.0,
                               base=0, pattern=[[1, P]], channel_multiplier=-1).then_inc(s_const, 1)
            pool.memset(pad_row[:, TOKEN:TOKEN + 1].bitcast(U32), NOBODY).then_inc(s_const, 1)
            pool.wait_ge(s_wld, WEIGHTS)

            def step(norm, project, attend, merge, route):
                if norm:
                    pool.wait_ge(s_mv1, n(norm, k=1))
                    pool.tensor_tensor(ve1[:, :], mv1[:, 1:2], eps_col[:, :], ALU.add).then_inc(s_ve1, 1)
                    pool.wait_ge(s_ve1, n(norm, k=1))
                    pool.tensor_tensor(rstd1[:, :], ve1[:, :], neg_half[:, :], ALU.pow).then_inc(s_rstd1, 1)
                if merge:
                    pool.wait_ge(s_res, n(merge, k=1))
                    pool.wait_ge(s_rz, n(merge, k=1))
                    pool.tensor_tensor(att[:, :], res[:, :], rz[:, :], ALU.mult).then_inc(s_att, 1)
                if attend:
                    pool.wait_ge(s_zinv, n(attend, k=1))
                    pool.tensor_tensor(z_prod[:, :], z[:, :], z_inv[:, :], ALU.mult).then_inc(s_zprod, 1)
                if project:
                    if tile_no(project) >= 2:
                        pool.wait_ge(s_x1s, n(project, k=-1))
                    pool.wait_ge(s_x[slot(project)], 16 * half(project) + 16)
                    pool.tensor_tensor(xb[:, slot(project), :], x_in[:, slot(project), :], bias_o[:, :],
                                       ALU.add).then_inc(s_xb, 1)
                if merge:
                    pool.wait_ge(s_mv2, n(merge, k=1))
                    pool.tensor_tensor(ve2[:, :], row[:, slot(merge), MEAN + 1:MEAN + 2], eps_col[:, :],
                                       ALU.add).then_inc(s_ve2, 1)
                    pool.wait_ge(s_ve2, n(merge, k=1))
                    pool.tensor_tensor(row[:, slot(merge), RSTD:RSTD + 1], ve2[:, :], neg_half[:, :],
                                       ALU.pow).then_inc(s_rstd2, 1)
                    pool.tensor_copy(row[:, slot(merge), TOKEN:TOKEN + 1].bitcast(U32),
                                     tokens[:, bass.ds(n(merge), 1)]).then_inc(s_token, 1)
                if route:
                    pool.wait_ge(s_place, n(route, k=1))
                    pool.wait_ge(s_token, n(route, k=1))
                    pool.tensor_tensor(onehots[:, :], onehots[:, :], onehot[:, :], ALU.add).then_inc(s_hots, 1)
                    pool.indirect_dma_start(buckets, bass.IndirectOffsetOnAxis(place[:, slot(route):slot(route) + 1], 0),
                                            row[:, slot(route), :], None).then_inc(s_bucket[slot(route)], 16)

            schedule(pool, step)

            pool.wait_ge(s_count, 3)
            for e in range(E):
                pool.indirect_dma_start(buckets, bass.IndirectOffsetOnAxis(pad_place[:, e:e + 1], 0),
                                        pad_row[:, :], None).then_inc(s_pad, 16)

            def slot_step(load, transpose, multiply):
                if multiply:
                    pool.wait_ge(s_sums, m(multiply, k=1))
                    pool.wait_ge(s_tok2, m(multiply, k=1))
                if load:
                    r = load[1] % RING
                    pool.wait_ge(s_rows2[r], 16 * turn(load) + 16)
                    if slot_no_of(load) >= RING:
                        pool.wait_ge(s_outs[r], 16 * turn(load))
                    pool.tensor_tensor(token[:, r:r + 1], rows2[:, r, TOKEN:TOKEN + 1].bitcast(U32), zero_u[:, :],
                                       ALU.add).then_inc(s_tok2, 1)
                if multiply:
                    r = multiply[1] % RING
                    pool.indirect_dma_start(out.rearrange("t p n -> (t p) n"),
                                            bass.IndirectOffsetOnAxis(token[:, r:r + 1], 0), sums[:, r, :], None,
                                            bounds_check=TOKENS - 1, oob_is_err=False).then_inc(s_outs[r], 16)

            slot_schedule(pool, slot_step)
            for r in range(RING):
                pool.wait_ge(s_outs[r], 16 * (SLOTS // RING))

        @block.scalar
        def _(act):
            act.preload_act_table_set("natural_log_exp_and_others")
            act.wait_ge(s_wld, WEIGHTS)
            act.activation(wqkv_hi[:, :, :], stage_small[:, :, 0:3 * D], ACT.Copy).then_inc(s_hi, 1)
            act.activation(wo_hi[:, :, :], stage_small[:, :, 3 * D:4 * D], ACT.Copy).then_inc(s_hi, 1)
            act.wait_ge(s_const, POOL_MADE)
            act.activation(ones_row[:, :], tri[0:1, :], ACT.Copy).then_inc(s_hi, 1)
            act.wait_ge(s_cst, MADE)

            def step(norm, project, attend, merge, route):
                if attend:
                    if tile_no(attend) >= 1:
                        act.wait_ge(s_rz, n(attend))
                    act.wait_ge(s_z, n(attend, k=1))
                    act.activation(z[:, :], b_z[:, 0:D], ACT.Copy).then_inc(s_zc, 1)
                    act.activation(z_ln[:, :], b_z[:, 0:D], ACT.Ln).then_inc(s_zc, 1)
                    act.wait_ge(s_zc, n(attend, 2, 2))
                    act.activation(z_inv[:, :], z_ln[:, :], ACT.Exp, scale=-1.0).then_inc(s_zinv, 1)
                if project:
                    act.wait_ge(s_qkb, n(project, k=1))
                    act.activation(qk_exp[:, :], qk[:, :], ACT.Exp).then_inc(s_exp, 1)
                if route:
                    act.wait_ge(s_x2T, n(route, k=1))
                    act.activation(x2_f[:, :], b_z[:, 0:D], ACT.Copy).then_inc(s_x2f, 1)
                if attend:
                    act.wait_ge(s_states, n(attend, k=1))
                    act.activation(state[C:2 * C, :, :], b_st[C:2 * C, 0:D].rearrange("p (a b) -> p a b", b=C),
                                   ACT.Copy).then_inc(s_state, 1)
                    act.activation(state[2 * C:P, :, :], b_st[2 * C:P, 0:D].rearrange("p (a b) -> p a b", b=C),
                                   ACT.Copy).then_inc(s_state, 1)
                if project:
                    act.activation(qk_pos[:, :], qk[:, :], ACT.Relu).then_inc(s_exp, 1)
                if route:
                    act.wait_ge(s_hid, n(route, k=1))
                    act.activation(hT[:, :], b_y[0:FF, 0:P], ACT.Relu, bias=bias_1[:, :]).then_inc(s_hT, 1)
                if norm:
                    act.wait_ge(s_t1, n(norm, k=1))
                    act.activation(xc_hi[:, :], b_xc[:, :], ACT.Copy).then_inc(s_xch, 1)
                if norm and tile_no(norm) == 2:
                    act.wait_ge(s_eld, EXPERTS)
                    act.activation(be_hi[:, :, :], stage_be[:, :, :], ACT.Copy).then_inc(s_ehi, 1)
                if norm and 2 <= tile_no(norm) < 2 + KC:
                    piece = tile_no(norm) - 2
                    act.activation(we_hi[:, piece, :, :], stage_w[:, piece, :, :], ACT.Copy).then_inc(s_ehi, 1)
                if merge:
                    act.wait_ge(s_attT, n(merge, k=1))
                    act.activation(attT_hi[:, :], b_sc[:, 0:D], ACT.Copy).then_inc(s_ath, 1)
                if project:
                    act.wait_ge(s_qkT, n(project, k=1))
                    for h in range(2):
                        act.activation(qsel[:, slot(project), :, h, :], qkT[:, 0, :, :], ACT.Copy,
                                       scale=head_sel[:, h:h + 1]).then_inc(s_qsel, 1)
                if attend:
                    act.wait_ge(s_o, n(attend, k=1))
                    act.activation(res0[:, :, :],
                                   b_o[:, :].rearrange("p (a h b) -> p a h b", h=2, b=C)[:, :, 0, :],
                                   ACT.Copy, scale=head_sel[:, 0:1]).then_inc(s_res0, 1)

            schedule(act, step)

            def slot_step(load, transpose, multiply):
                if transpose:
                    act.wait_ge(s_x3T, m(transpose, k=1))
                    act.activation(x3_hi[:, transpose[1] % 2, :], (b_xc, b_sc)[transpose[1] % 2][:, 0:D],
                                   ACT.Copy).then_inc(s_x3h, 1)

            slot_schedule(act, slot_step)

        @block.vector
        def _(dve):
            dve.memset(head_sel[:, 0:1], 0.0).then_inc(s_cst, 1)
            dve.memset(head_sel[:, 1:2], 1.0).then_inc(s_cst, 1)
            dve.memset(one_e[:, :], 1.0).then_inc(s_cst, 1)
            dve.wait_ge(s_cst, 3)
            for c in range(NCH):
                dve.memset(head_sel[C * c:C * c + HD, 0:1], 1.0)
                last = dve.memset(head_sel[C * c:C * c + HD, 1:2], 0.0)
            last.then_inc(s_cst, 1)
            dve.wait_ge(s_const, POOL_MADE)
            for c in range(NCH):
                for h in range(2 * PAIRS):
                    last = dve.tensor_copy(chunk_mask[C * c:C * c + C, h, :], tri[C * c:C * c + C, C * c:C * c + C])
            last.then_inc(s_cst, 1)
            dve.wait_ge(s_hi, 3)
            dve.tensor_tensor(wqkv_lo[:, :, :], stage_small[:, :, 0:3 * D], wqkv_hi[:, :, :].bitcast(F32),
                              ALU.subtract).then_inc(s_cst, 1)
            dve.tensor_tensor(wo_lo[:, :, :], stage_small[:, :, 3 * D:4 * D], wo_hi[:, :, :].bitcast(F32),
                              ALU.subtract).then_inc(s_cst, 1)
            dve.wait_ge(s_cst, MADE)

            def step(norm, project, attend, merge, route):
                if route:
                    dve.wait_ge(s_rstd2, n(route, k=1))
                    dve.tensor_scalar(x2n[:, :], row[:, slot(route), 0:D], row[:, slot(route), MEAN:MEAN + 1],
                                      row[:, slot(route), RSTD:RSTD + 1], ALU.subtract, ALU.mult).then_inc(s_x2n, 1)
                if project:
                    dve.wait_ge(s_qk, n(project, k=1))
                    dve.tensor_tensor(qk[:, :], b_qk[:, :], bias_qkv[:, 0:2 * D], ALU.add).then_inc(s_qkb, 1)
                if norm:
                    dve.wait_ge(s_x[slot(norm)], 16 * half(norm) + 16)
                    dve.bn_stats(st1[:, :], x_in[:, slot(norm), :]).then_inc(s_st1, 1)
                    dve.wait_ge(s_st1, n(norm, k=1))
                if project:
                    dve.wait_ge(s_v, n(project, k=1))
                    dve.tensor_tensor(v[:, slot(project), :], b_v[:, 0:D], bias_qkv[:, 2 * D:3 * D],
                                      ALU.add).then_inc(s_vb, 1)
                if norm:
                    dve.bn_aggr(mv1[:, :], st1[:, :]).then_inc(s_mv1, 1)
                if norm:
                    dve.wait_ge(s_rstd1, n(norm, k=1))
                    if tile_no(norm) >= 1:
                        dve.wait_ge(s_t1, n(norm))
                    dve.tensor_scalar(xn[:, :], x_in[:, slot(norm), :], mv1[:, 0:1], rstd1[:, 0:1],
                                      ALU.subtract, ALU.mult).then_inc(s_xn, 1)
                if attend:
                    dve.wait_ge(s_sc, n(attend, k=1))
                    dve.tensor_tensor(scores[:, :, :, :].rearrange("p a h b -> p (a h b)"), b_sc[:, :],
                                      chunk_mask[:, :, :].rearrange("p a b -> p (a b)"), ALU.mult).then_inc(s_scores, 1)
                if project:
                    dve.wait_ge(s_exp, n(project, 2, 2))
                    dve.scalar_tensor_tensor(qkp[:, :], qk_exp[:, :], 1.0, qk_pos[:, :], ALU.min, ALU.add).then_inc(s_qkp, 1)
                if route:
                    dve.wait_ge(s_lgp, n(route, k=1))
                    dve.tensor_tensor(logits[:, :], b_z[:, 0:E], bias_2[:, :], ALU.add).then_inc(s_pick, 1)
                    dve.wait_ge(s_pick, n(route, 3, 1))
                if merge:
                    dve.wait_ge(s_ath, n(merge, k=1))
                    dve.tensor_tensor(attT_lo[:, :], b_sc[:, 0:D], attT_hi[:, :].bitcast(F32), ALU.subtract).then_inc(s_atl, 1)
                if route:
                    dve.max(top[:, :], logits[:, :]).then_inc(s_pick, 1)
                    dve.wait_ge(s_pick, n(route, 3, 2))
                if project:
                    dve.wait_ge(s_qkp, n(project, k=1))
                    dve.transpose(qkT[:, :, :, :].rearrange("p q a b -> p (q a b)"), qkp[:, :]).then_inc(s_qkT, 1)
                if route:
                    dve.max_index(pick[:, :], top[:, :], logits[:, :]).then_inc(s_pick, 1)
                if norm:
                    dve.wait_ge(s_xch, n(norm, k=1))
                    dve.tensor_tensor(xc_lo[:, :], b_xc[:, :], xc_hi[:, :].bitcast(F32), ALU.subtract).then_inc(s_xcl, 1)
                if route:
                    if tile_no(route) >= 1:
                        dve.wait_ge(s_hots, n(route))
                    dve.wait_ge(s_pick, n(route, 3, 3))
                    dve.tensor_scalar(onehot[:, :], iota8[:, :], pick[:, 0:1], None, ALU.is_equal).then_inc(s_hot, 1)
                if norm and tile_no(norm) == 3:
                    dve.wait_ge(s_ehi, 1)
                    dve.tensor_tensor(be_lo[:, :, :], stage_be[:, :, :], be_hi[:, :, :].bitcast(F32),
                                      ALU.subtract).then_inc(s_elo, 1)
                if norm and 3 <= tile_no(norm) < 3 + KC:
                    piece = tile_no(norm) - 3
                    dve.wait_ge(s_ehi, 2 + piece)
                    dve.tensor_tensor(we_lo[:, piece, :, :], stage_w[:, piece, :, :], we_hi[:, piece, :, :].bitcast(F32),
                                      ALU.subtract).then_inc(s_elo, 1)
                if merge:
                    dve.wait_ge(s_y, n(merge, k=1))
                    dve.wait_ge(s_xb, n(merge, k=1))
                    if tile_no(merge) >= 2:
                        dve.wait_ge(s_bucket[slot(merge)], 16 * half(merge))
                    dve.tensor_tensor(row[:, slot(merge), 0:D], b_y[:, 0:D], xb[:, slot(merge), :], ALU.add).then_inc(s_x1s, 1)
                    dve.wait_ge(s_x1s, n(merge, k=1))
                    dve.bn_stats(st2[:, :], row[:, slot(merge), 0:D]).then_inc(s_st2, 1)
                    dve.wait_ge(s_st2, n(merge, k=1))
                if attend:
                    dve.wait_ge(s_res0, n(attend, k=1))
                    dve.scalar_tensor_tensor(resT[:, :, :],
                                             b_o[:, :].rearrange("p (a h b) -> p a h b", h=2, b=C)[:, :, 1, :],
                                             head_sel[:, 1:2], res0[:, :, :], ALU.mult, ALU.add).then_inc(s_resT, 1)
                if merge:
                    dve.bn_aggr(row[:, slot(merge), MEAN:MEAN + 2], st2[:, :]).then_inc(s_mv2, 1)
                if attend:
                    dve.wait_ge(s_zprod, n(attend, k=1))
                    dve.scalar_tensor_tensor(rz[:, :], z_prod[:, :], 2.0, z_inv[:, :], ALU.subtract, ALU.mult,
                                             reverse0=True).then_inc(s_rz, 1)
                    dve.wait_ge(s_resT, n(attend, k=1))
                    dve.transpose(res[:, :], resT[:, :, :].rearrange("p a b -> p (a b)")).then_inc(s_res, 1)
                if route:
                    dve.wait_ge(s_ranked, n(route, k=1))
                    dve.scalar_tensor_tensor(ranked[:, :], b_v[:, D:D + E], 1.0, onehot[:, :], ALU.mult, ALU.mult,
                                             accum_out=rank[:, :]).then_inc(s_rank, 1)
                    dve.wait_ge(s_rank, n(route, k=1))
                    dve.tensor_scalar(place[:, slot(route):slot(route) + 1], pick[:, 0:1], float(CAP), rank[:, 0:1],
                                      ALU.mult, ALU.add).then_inc(s_place, 1)

            schedule(dve, step)

            done = [0]

            def chain(ins):
                done[0] += 1
                ins.then_inc(s_fill, 1)
                dve.wait_ge(s_fill, done[0])

            dve.wait_ge(s_count, 1)
            dve.tensor_copy(count[:, :], b_v[:, 0:E]).then_inc(s_count, 1)
            dve.wait_ge(s_count, 2)
            dve.tensor_tensor(pad_place[:, :], count[:, :], pad_at[:, :], ALU.add).then_inc(s_count, 1)
            for e in range(E):
                chain(dve.tensor_scalar(over[:, :], multiples[:, :], count[0:1, e:e + 1], None, ALU.is_lt, ALU.add,
                                        accum_out=fill[:, e:e + 1]))
            chain(dve.tensor_tensor_scan(fill_sum[:, :], one_e[:, :], fill[:, :], 0.0, ALU.mult, ALU.add))
            chain(dve.tensor_scalar(jump[:, :], fill[:, :], float(-P), float(CAP), ALU.mult, ALU.add))
            chain(dve.tensor_scalar(slot_row[:, :], slot_no[:, :], float(P), None, ALU.mult))
            chain(dve.memset(slot_e[:, :], 0.0))
            for e in range(E - 1):
                chain(dve.tensor_scalar(step_row[:, :], slot_no[:, :], fill_sum[:, e:e + 1], jump[:, e:e + 1],
                                        ALU.is_ge, ALU.mult))
                chain(dve.tensor_tensor(slot_row[:, :], slot_row[:, :], step_row[:, :], ALU.add))
                chain(dve.scalar_tensor_tensor(slot_e[:, :], slot_no[:, :], fill_sum[:, e:e + 1], slot_e[:, :],
                                               ALU.is_ge, ALU.add))
            chain(dve.tensor_scalar(slot_used[:, :], slot_no[:, :], fill_sum[:, E - 1:E], None, ALU.is_lt))
            chain(dve.scalar_tensor_tensor(slot_row[:, :], slot_row[:, :], float(SPARE), slot_used[:, :],
                                           ALU.subtract, ALU.mult))
            chain(dve.tensor_scalar(row_of[:, :], slot_row[:, :], float(SPARE), None, ALU.add))
            chain(dve.memset(expert_of[:, 0:2], 0))
            chain(dve.tensor_copy(expert_of[:, 2:2 + SLOTS], slot_e[:, :]))
            assert done[0] == FILL_STEPS

            def slot_step(load, transpose, multiply):
                if load:
                    r = load[1] % RING
                    dve.wait_ge(s_rows2[r], 16 * turn(load) + 16)
                    if slot_no_of(load) >= 2:
                        dve.wait_ge(s_x3T, m(load, k=-1))
                    dve.tensor_scalar(x3n[:, load[1] % 2, :], rows2[:, r, 0:D], rows2[:, r, MEAN:MEAN + 1],
                                      rows2[:, r, RSTD:RSTD + 1], ALU.subtract, ALU.mult).then_inc(s_x3n, 1)
                if transpose:
                    dve.wait_ge(s_x3h, m(transpose, k=1))
                    dve.tensor_tensor(x3_lo[:, transpose[1] % 2, :], (b_xc, b_sc)[transpose[1] % 2][:, 0:D],
                                      x3_hi[:, transpose[1] % 2, :].bitcast(F32), ALU.subtract).then_inc(s_x3l, 1)
                if multiply:
                    r = multiply[1] % RING
                    dve.wait_ge(s_prod, m(multiply, k=1))
                    if slot_no_of(multiply) >= RING:
                        dve.wait_ge(s_outs[r], 16 * turn(multiply))
                    dve.tensor_tensor(sums[:, r, :], (b_qk, b_v)[multiply[1] % 2][:, 0:D], rows2[:, r, 0:D],
                                      ALU.add).then_inc(s_sums, 1)

            slot_schedule(dve, slot_step)

        @block.tensor
        def _(pe):
            pe.wait_ge(s_const, POOL_MADE)
            pe.wait_ge(s_cst, MADE)
            pe.wait_ge(s_wld, WEIGHTS)

            def split_product(dst, lhs_hi, lhs_lo, rhs_hi, rhs_lo, last_of_group=True):
                parts = [(k, a, b) for k in range(KC) for a, b in
                         ((lhs_hi, rhs_hi), (lhs_hi, rhs_lo), (lhs_lo, rhs_hi))]
                for i, (k, a, b) in enumerate(parts):
                    last = pe.matmul(dst, a(k), b(k), start=(i == 0), stop=(last_of_group and i == len(parts) - 1))
                return last

            def rows(c):
                return slice(C * c, C * c + C)

            def step(norm, project, attend, merge, route):
                a = slot(attend) if attend else 0
                def score(pairs):
                    for p in pairs:
                        for c in range(NCH):
                            last = pe.matmul(b_sc[rows(c), 2 * C * p:2 * C * (p + 1)], qkT[rows(c), 1, p, :],
                                             qsel[rows(c), a, p, :, :], start=True, stop=True)
                    return last

                def attention(pairs):
                    for p in pairs:
                        for c in range(NCH):
                            last = pe.matmul(b_o[rows(c), 2 * C * p:2 * C * (p + 1)], v[rows(c), a, C * p:C * p + C],
                                             scores[rows(c), p, :, :], start=True, stop=(c == 0))
                        for c in range(1, NCH):
                            last = pe.matmul(b_o[rows(c), 2 * C * p:2 * C * (p + 1)], state[rows(c), p, :],
                                             qsel[rows(c), a, p, :, :], start=False, stop=True)
                    return last

                def project_to(dst, of_ctx, first):
                    at = D * of_ctx
                    return split_product(dst, lambda k: xc_hi[:, at + k * P:at + (k + 1) * P],
                                         lambda k: xc_lo[:, at + k * P:at + (k + 1) * P],
                                         lambda k: wqkv_hi[:, k, first:first + D], lambda k: wqkv_lo[:, k, first:first + D])

                if attend:
                    pe.wait_ge(s_qkp, n(attend, k=1))
                    if tile_no(attend) >= 3:
                        pe.wait_ge(s_pick, n(attend, 3, -8))
                    pe.matmul(b_z[:, 0:D], tri[:, :], qkp[:, 0:D], start=True, stop=True).then_inc(s_z, 1)
                if attend:
                    pe.wait_ge(s_qkT, n(attend, k=1))
                    pe.wait_ge(s_qsel, n(attend, 2, 2))
                if project:
                    pe.wait_ge(s_xcl, n(project, k=1))
                    if tile_no(project) >= 1:
                        pe.wait_ge(s_qkb, n(project))
                    project_to(b_qk[:, 0:D], 0, 0)
                if project:
                    project_to(b_qk[:, D:2 * D], 1, D).then_inc(s_qk, 1)
                if project:
                    if tile_no(project) >= 4:
                        pe.wait_ge(s_rank, n(project, k=-3))
                    project_to(b_v[:, 0:D], 1, 2 * D).then_inc(s_v, 1)
                if attend:
                    score(range(0, PAIRS // 2))
                if attend:
                    pe.wait_ge(s_vb, n(attend, k=1))
                    for p in range(PAIRS):
                        for c in range(NCH - 1, 0, -1):
                            last = pe.matmul(b_st[rows(c), C * p:C * p + C], qkp[0:C * c, D + C * p:D + C * p + C],
                                             v[0:C * c, a, C * p:C * p + C], start=True, stop=True)
                    last.then_inc(s_states, 1)
                if route:
                    pe.wait_ge(s_x2n, n(route, k=1))
                    if attend:
                        pe.wait_ge(s_zc, n(attend, 2, 2))
                    for k in range(KC):
                        last = pe.transpose(b_z[:, k * P:(k + 1) * P], x2n[:, k * P:(k + 1) * P], ident[:, :])
                    last.then_inc(s_x2T, 1)
                if attend:
                    score(range(PAIRS // 2, PAIRS)).then_inc(s_sc, 1)
                if route:
                    pe.wait_ge(s_x2f, n(route, k=1))
                    for k in range(KC):
                        last = pe.matmul(b_y[0:FF, 0:P], w1_sb[:, k, :], x2_f[:, k * P:(k + 1) * P],
                                         start=(k == 0), stop=(k == KC - 1))
                    last.then_inc(s_hid, 1)
                if norm:
                    pe.wait_ge(s_xn, n(norm, k=1))
                    pe.wait_ge(s_ctx[slot(norm)], 16 * half(norm) + 16)
                    for k in range(KC):
                        pe.transpose(b_xc[:, k * P:(k + 1) * P], xn[:, k * P:(k + 1) * P], ident[:, :])
                    for k in range(KC):
                        last = pe.transpose(b_xc[:, D + k * P:D + (k + 1) * P],
                                            ctx_in[:, slot(norm), k * P:(k + 1) * P], ident[:, :])
                    last.then_inc(s_t1, 1)
                if attend:
                    pe.wait_ge(s_state, n(attend, 2, 2))
                    if tile_no(attend) >= 1:
                        pe.wait_ge(s_resT, n(attend))
                    pe.wait_ge(s_scores, n(attend, k=1))
                if merge:
                    pe.wait_ge(s_att, n(merge, k=1))
                    for k in range(KC):
                        last = pe.transpose(b_sc[:, k * P:(k + 1) * P], att[:, k * P:(k + 1) * P], ident[:, :])
                    last.then_inc(s_attT, 1)
                if route:
                    pe.wait_ge(s_hT, n(route, k=1))
                    pe.matmul(b_z[:, 0:E], hT[:, :], w2_sb[:, :], start=True, stop=True).then_inc(s_lgp, 1)
                if attend:
                    attention(range(0, PAIRS // 2))
                if merge:
                    pe.wait_ge(s_atl, n(merge, k=1))
                    split_product(b_y[:, 0:D],
                                  lambda k: attT_hi[:, k * P:(k + 1) * P], lambda k: attT_lo[:, k * P:(k + 1) * P],
                                  lambda k: wo_hi[:, k, :], lambda k: wo_lo[:, k, :]).then_inc(s_y, 1)
                if attend:
                    attention(range(PAIRS // 2, PAIRS)).then_inc(s_o, 1)
                if route:
                    pe.wait_ge(s_hot, n(route, k=1))
                    if project:
                        pe.wait_ge(s_vb, n(project, k=1))
                    if tile_no(route) >= 1:
                        pe.wait_ge(s_hots, n(route))
                    pe.matmul(b_v[:, D:D + E], before[:, :], onehot[:, :], start=True, stop=False)
                    pe.matmul(b_v[:, D:D + E], ones[:, :], onehots[:, :], start=False, stop=True).then_inc(s_ranked, 1)

            schedule(pe, step)
            pe.wait_ge(s_hots, TILES)
            pe.wait_ge(s_rank, TILES)
            pe.matmul(b_v[:, 0:E], ones[:, :], onehots[:, :], start=True, stop=True).then_inc(s_count, 1)
            pe.wait_ge(s_fill, FILL_STEPS)

            pe.wait_ge(s_elo, 1 + KC)
            experts = []

            def load_experts(first, how_many):
                experts.extend(nc.values_load_multi_w_load_instructions(
                    expert_of[0:1, bass.ds(m(first, k=2), how_many)], [mybir.EngineType.PE], min_val=0, max_val=E - 1,
                    skip_runtime_bounds_check_because="the tables are computed on the chip within these bounds")[1])

            def slot_step(load, transpose, multiply):
                if not multiply and load:
                    experts.pop(0)
                if transpose:
                    h = transpose[1] % 2
                    pe.wait_ge(s_x3n, m(transpose, k=1))
                    if slot_no_of(transpose) >= 2:
                        pe.wait_ge(s_x3l, m(transpose, k=-1))
                    for k in range(KC):
                        last = pe.transpose((b_xc, b_sc)[h][:, k * P:(k + 1) * P], x3n[:, h, k * P:(k + 1) * P], ident[:, :])
                    last.then_inc(s_x3T, 1)
                if multiply:
                    h = multiply[1] % 2
                    e = experts.pop(0)
                    pe.wait_ge(s_x3l, m(multiply, k=1))
                    if slot_no_of(multiply) >= 2:
                        pe.wait_ge(s_sums, m(multiply, k=-1))
                    dst = (b_qk, b_v)[h][:, 0:D]
                    split_product(dst,
                                  lambda k: x3_hi[:, h, k * P:(k + 1) * P], lambda k: x3_lo[:, h, k * P:(k + 1) * P],
                                  lambda k: we_hi[:, k, bass.ds(e, 1), :], lambda k: we_lo[:, k, bass.ds(e, 1), :],
                                  last_of_group=False)
                    pe.matmul(dst, ones_row[:, :], be_hi[0:1, bass.ds(e, 1), :], start=False, stop=False)
                    pe.matmul(dst, ones_row[:, :], be_lo[0:1, bass.ds(e, 1), :], start=False, stop=True)\
                        .then_inc(s_prod, 1)

            slot_schedule(pe, slot_step, load_experts)


_INS = ["x", "ctx_1024", "L0_xattn_Wq", "L0_xattn_bq", "L0_xattn_Wk", "L0_xattn_bk", "L0_xattn_Wv",
        "L0_xattn_bv", "L0_xattn_Wo", "L0_xattn_bo", "L0_ffn_W1", "L0_ffn_b1", "L0_ffn_W2", "L0_ffn_b2",
        "L0_ffn_expert_W", "L0_ffn_expert_b"]


def kernel(**inputs):
    import numpy as np
    import concourse.bacc as bacc
    from concourse.bass_utils import run_bass_kernel_spmd

    nc = bacc.Bacc("TRN2", target_bir_lowering=False, num_devices=1)
    arrays, args = {}, []
    for name in _INS:
        a = np.ascontiguousarray(inputs[name])
        arrays[f"in_{name}"] = a
        args.append(nc.dram_tensor(f"in_{name}", a.shape, mybir.dt.from_np(a.dtype), kind="ExternalInput").ap())
    out = nc.dram_tensor("out", arrays["in_x"].shape, F32, kind="ExternalOutput").ap()
    build(nc, *args, out)
    return run_bass_kernel_spmd(nc, [arrays], core_ids=[0]).results[0]["out"]
```
